# Optimizing a Trainium2 kernel written in Bass

```python
import numpy as np
import jax
import jax.numpy as jnp

def _softmax(x, axis=-1):
    return jax.nn.softmax(x, axis=axis)

def _gelu(x):
    return jax.nn.gelu(x, approximate=True)

def _silu(x):
    return jax.nn.silu(x)

def _sigmoid(x):
    return jax.nn.sigmoid(x)

def _layernorm(x, axis=-1, eps=1e-05):
    m = jnp.mean(x, axis=axis, keepdims=True)
    v = jnp.var(x, axis=axis, keepdims=True)
    return (x - m) / jnp.sqrt(v + eps)

def _scatter_add(tgt, idx, src, axis=0):
    return tgt.at[idx].add(src)

def _segment_sum(src, seg, n):
    return jax.ops.segment_sum(src, seg, n)
kernel_name = 'mk_gps_d1_gnn_r8_9eb382'

def setup_inputs(seed: int=0):
    np.random.seed(seed)
    _w = jnp.asarray

    def _rec_inputs():
        import jax
        import jax.numpy as jnp
        _gk = jax.random.key(seed)
        x = -0.0001126 + 1 * jax.random.normal(jax.random.fold_in(_gk, 1), (1250, 768), jnp.float32)
        src = jax.random.randint(jax.random.fold_in(_gk, 2), (20000,), 0, 1250, jnp.int32)
        dst = jax.random.randint(jax.random.fold_in(_gk, 3), (20000,), 0, 1250, jnp.int32)
        _o = jnp.argsort(dst, stable=True)
        src = src[_o]
        dst = dst[_o]
        return (x, src, dst)
    x, src, dst = _rec_inputs()

    def _L0_gnn_setup():
        import jax, jax.numpy as jnp
        import numpy as np
        N_NODES = 1250
        key = jax.random.key(seed)
        k1, k2, k3 = jax.random.split(key, 3)
        x = jax.random.normal(k1, (N_NODES, 768), dtype=jnp.float32)
        edge_index = jax.random.randint(k2, (2, 12500), 0, N_NODES, dtype=jnp.int32)
        W = jax.random.normal(k3, (768, 768), dtype=jnp.float32) * (1.0 / np.sqrt(768))
        b = jnp.zeros((768,), dtype=jnp.float32)
        return {'x': x, 'edge_index': edge_index, 'W': W, 'b': b}
    _L0_gnn_all = _L0_gnn_setup()
    _L0_gnn_in = {k: v for k, v in _L0_gnn_all.items() if k in ('W', 'b')}
    del _L0_gnn_all

    def _L0_mix_setup():
        import jax, jax.numpy as jnp
        import numpy as np
        DIM = 768
        NUM_HEADS = 12
        HEAD_DIM = DIM // NUM_HEADS
        SCALE = HEAD_DIM ** (-0.5)
        key = jax.random.key(seed)
        ks = jax.random.split(key, 5)
        B, N = (4, 1024)
        s = DIM ** (-0.5)
        return {'x': jax.random.normal(ks[0], (B, N, DIM), dtype=jnp.float32), 'w_qkv': jax.random.normal(ks[1], (DIM, 3 * DIM), dtype=jnp.float32) * s, 'b_qkv': jnp.zeros((3 * DIM,), dtype=jnp.float32), 'w_proj': jax.random.normal(ks[2], (DIM, DIM), dtype=jnp.float32) * s, 'b_proj': jnp.zeros((DIM,), dtype=jnp.float32)}
    _L0_mix_all = _L0_mix_setup()
    _L0_mix_in = {k: v for k, v in _L0_mix_all.items() if k in ('w_qkv', 'b_qkv', 'w_proj', 'b_proj')}
    del _L0_mix_all

    def _L0_ffn_setup():
        import jax, jax.numpy as jnp
        import numpy as np
        CAPACITY_FACTOR = 1.25
        key = jax.random.key(seed)
        ks = jax.random.split(key, 5)
        B, S, D, F, E = (8, 256, 768, 384, 8)
        return {'x': jax.random.normal(ks[0], (B, S, D), jnp.float32), 'switch_w': jax.random.normal(ks[1], (D, E), jnp.float32) * 0.02, 'switch_b': jnp.zeros((E,), jnp.float32), 'w1': jax.random.normal(ks[2], (E, D, F), jnp.float32) * 0.02, 'b1': jnp.zeros((E, F), jnp.float32), 'w2': jax.random.normal(ks[3], (E, F, D), jnp.float32) * 0.02, 'b2': jnp.zeros((E, D), jnp.float32)}
    _L0_ffn_all = _L0_ffn_setup()
    _L0_ffn_in = {k: v for k, v in _L0_ffn_all.items() if k in ('switch_w', 'switch_b', 'w1', 'b1', 'w2', 'b2')}
    del _L0_ffn_all
    return {'x': x, 'src': src, 'dst': dst, 'L0_gnn_W': _L0_gnn_in['W'], 'L0_gnn_b': _L0_gnn_in['b'], 'L0_mix_w_qkv': _L0_mix_in['w_qkv'], 'L0_mix_b_qkv': _L0_mix_in['b_qkv'], 'L0_mix_w_proj': _L0_mix_in['w_proj'], 'L0_mix_b_proj': _L0_mix_in['b_proj'], 'L0_ffn_switch_w': _L0_ffn_in['switch_w'], 'L0_ffn_switch_b': _L0_ffn_in['switch_b'], 'L0_ffn_w1': _L0_ffn_in['w1'], 'L0_ffn_b1': _L0_ffn_in['b1'], 'L0_ffn_w2': _L0_ffn_in['w2'], 'L0_ffn_b2': _L0_ffn_in['b2']}

def reference(x, src, dst, L0_gnn_W, L0_gnn_b, L0_mix_w_qkv, L0_mix_b_qkv, L0_mix_w_proj, L0_mix_b_proj, L0_ffn_switch_w, L0_ffn_switch_b, L0_ffn_w1, L0_ffn_b1, L0_ffn_w2, L0_ffn_b2):
    import jax
    import jax.numpy as jnp

    def _L0_gnn_ref(x, edge_index, W, b):
        import jax, jax.numpy as jnp
        import numpy as np
        N_NODES = 1250
        n = x.shape[0]
        loops = jnp.arange(n, dtype=edge_index.dtype)
        row = jnp.concatenate([edge_index[0], loops])
        col = jnp.concatenate([edge_index[1], loops])
        ones = jnp.ones(row.shape[0], dtype=x.dtype)
        deg = jax.ops.segment_sum(ones, col, num_segments=n)
        dinv = jnp.where(deg > 0, jax.lax.rsqrt(deg), 0.0)
        norm = dinv[row] * dinv[col]
        h = x @ W
        msg = h[row] * norm[:, None]
        out = jax.ops.segment_sum(msg, col, num_segments=n) + b
        return out

    def _L0_mix_ref(x, w_qkv, b_qkv, w_proj, b_proj):
        import jax, jax.numpy as jnp
        import numpy as np
        DIM = 768
        NUM_HEADS = 12
        HEAD_DIM = DIM // NUM_HEADS
        SCALE = HEAD_DIM ** (-0.5)
        B, N, C = x.shape
        H, D = (NUM_HEADS, HEAD_DIM)
        qkv = x @ w_qkv + b_qkv
        qkv = qkv.reshape(B, N, 3, H, D).transpose(2, 0, 3, 1, 4)
        q, k, v = (qkv[0] * SCALE, qkv[1], qkv[2])
        A = jnp.einsum('bhnd,bhmd->bhnm', q, k)
        numerator = 1.0 + A + 0.5 * A * A
        attn = numerator / numerator.sum(axis=-1, keepdims=True)
        out = jnp.einsum('bhnm,bhmd->bhnd', attn, v)
        out = out.transpose(0, 2, 1, 3).reshape(B, N, C)
        return out @ w_proj + b_proj

    def _L0_ffn_ref(x, switch_w, switch_b, w1, b1, w2, b2):
        import jax, jax.numpy as jnp
        import numpy as np
        CAPACITY_FACTOR = 1.25
        B, S, D = x.shape
        E = w1.shape[0]
        xf = x.reshape(-1, D)
        N = xf.shape[0]
        capacity = int(CAPACITY_FACTOR * N / E)
        probs = jax.nn.softmax(xf @ switch_w + switch_b, axis=-1)
        prob_max = jnp.max(probs, axis=-1)
        routes = jnp.argmax(probs, axis=-1)
        sort_idx = jnp.lexsort((-prob_max, routes))
        counts = jnp.bincount(routes, length=E)
        starts = jnp.concatenate([jnp.zeros((1,), counts.dtype), jnp.cumsum(counts)[:-1]])
        rank_sorted = jnp.arange(N) - starts[routes[sort_idx]]
        rank = jnp.zeros((N,), jnp.int32).at[sort_idx].set(rank_sorted.astype(jnp.int32))
        keep = rank < capacity
        dest_e = jnp.where(keep, routes, E)
        dest_c = jnp.where(keep, rank, 0)
        buf = jnp.zeros((E + 1, capacity, D), xf.dtype).at[dest_e, dest_c].set(xf)
        h = jax.nn.gelu(jnp.einsum('ecd,edf->ecf', buf[:E], w1) + b1[:, None, :], approximate=False)
        o = jnp.einsum('ecf,efd->ecd', h, w2) + b2[:, None, :]
        y_exp = o[routes, dest_c]
        y = jnp.where(keep[:, None], y_exp, xf)
        out = y * prob_max[:, None]
        return out.reshape(B, S, D)
    edge_index = jnp.stack([src, dst])
    xn = _layernorm(x, axis=-1)
    x = x + _L0_gnn_ref(xn, edge_index, L0_gnn_W, L0_gnn_b) + _L0_mix_ref(xn[None], L0_mix_w_qkv, L0_mix_b_qkv, L0_mix_w_proj, L0_mix_b_proj)[0]
    x = x + _L0_ffn_ref(_layernorm(x, axis=-1)[None], L0_ffn_switch_w, L0_ffn_switch_b, L0_ffn_w1, L0_ffn_b1, L0_ffn_w2, L0_ffn_b2)[0]
    return x

_drawn_inputs = setup_inputs


def setup_inputs(seed=0):
    import zlib

    import numpy as np

    out = dict(_drawn_inputs(seed))
    spreads = {'L0_gnn_b': (0.0, 0.1),
     'L0_mix_b_qkv': (0.0, 0.1),
     'L0_mix_b_proj': (0.0, 0.1),
     'L0_ffn_switch_b': (0.0, 0.1),
     'L0_ffn_b1': (0.0, 0.8),
     'L0_ffn_b2': (0.0, 0.344)}
    factors = {}
    for name, (base, spread) in spreads.items():
        noise = np.random.default_rng([zlib.crc32(name.encode()), seed]).standard_normal(out[name].shape)
        drawn = base * np.exp(spread * noise) if base else spread * noise
        out[name] = jnp.asarray(drawn.astype(out[name].dtype))
    for name, factor in factors.items():
        out[name] = (out[name] * factor).astype(out[name].dtype)
    return out
```

```python
from contextlib import ExitStack

import concourse.bass as bass
from concourse import mybir

F32 = mybir.dt.float32
F32R = mybir.dt.float32r
BF16 = mybir.dt.bfloat16
I32 = mybir.dt.int32
U32 = mybir.dt.uint32
ALU = mybir.AluOpType
ACT = mybir.ActivationFunctionType
AX = mybir.AxisListType

P = 128
N, D = 1250, 768
T, NT = 125, 10
KT = D // P
HALF = D // 2
H, HD = 12, 64
PAIRS = H // 2
SCALE = HD ** -0.5
EPS = 1e-5
CHUNKS = [(0, 418), (418, 416), (834, 416)]
CW = 418
EDGES = 20000
ET = EDGES // T
EC, EU = 16, ET // 16
EROWS = 80
CLEARED = 32
AGAIN = 256.0
E, F = 8, 384
FT = F // P
CAP = int(1.25 * N / E)
SLOTS = E * CAP
CAPP = CAP + 1
CTILES = [(0, 98), (98, 97)]
STEPS = 30
LAG = 3
RING = 3


class Chain:

    def __init__(self, eng, sem, base=0):
        self.eng, self.sem, self.base, self.n = eng, sem, base, 0

    def __call__(self, ins):
        self.n += 1
        ins.then_inc(self.sem, 1)
        self.eng.wait_ge(self.sem, self.base + self.n)


def at(start, size):
    return bass.ds(start, size)


def build(nc, x, src, dst, gnn_w, gnn_b, w_qkv, b_qkv, w_proj, b_proj, sw, sb_, w1, b1, w2, b2, out,
          counts, keyd, vdram, odram, rows, x1d):
    ctx = ExitStack()
    with ctx:
        def sem(name):
            return ctx.enter_context(nc.semaphore(name))

        def keep(name, shape, dt):
            return ctx.enter_context(nc.sbuf_tensor(name, shape, dt))

        def region(specs):
            with ExitStack() as inner:
                return [inner.enter_context(nc.sbuf_tensor(*s)) for s in specs]

        def left(stack, specs):
            return [stack.enter_context(nc.sbuf_tensor(*s)) for s in specs]

        def right(stack, specs):
            return [stack.enter_context(nc.sbuf_tensor(*s, side="right")) for s in specs]

        ps = ctx.enter_context(nc.psum_tensor("ps", [P, 8, 512], F32))

        ident = keep("ident", [P, P], F32)
        blocks = keep("blocks", [P, P], F32)
        ones2 = keep("ones2", [T, 2], F32)
        later = keep("later", [T, T], F32)
        iota_i = keep("iota_i", [T, 32], I32)
        iota_f = keep("iota_f", [T, 32], F32)
        countc = keep("countc", [T, ET], F32)
        idxf = keep("idxf", [T, ET], F32)
        icur = keep("icur", [T, 2], U32)
        vcur = keep("vcur", [T, 2], F32)
        stats = keep("stats", [T, NT, 2, 6], F32)
        mv = keep("mv", [T, NT, 2], F32)
        rs = keep("rs", [T, 4, NT], F32)
        bcols = keep("bcols", [P, 3, PAIRS + 1], F32)
        pbias = keep("pbias", [P, 2], F32)
        dinv = keep("dinv", [T, NT], F32)
        dtmp = keep("dtmp", [T, 4, NT], F32)
        swk, sbr = keep("swk", [P, KT, E], F32), keep("sbr", [T, E], F32)
        lg = keep("lg", [T, 6, NT, E], F32)
        rt = keep("rt", [T, 10, NT], F32)
        ohb = keep("ohb", [T, NT, E], BF16)
        slots = keep("slots", [T, NT], U32)
        b1c, b1cur = keep("b1c", [P, E, FT], F32), keep("b1cur", [P, 2, FT], F32)

        x_in = [sem(f"x_in{i}") for i in range(NT)]
        e_in, b_in = sem("e_in"), sem("b_in")
        key_out, kb_in = sem("key_out"), [sem("kb_in0"), sem("kb_in1")]
        r_zero = sem("r_zero")
        w_in = [sem("w_in0"), sem("w_in1")]
        v_store = [sem("v_store0"), sem("v_store1")]
        o_store = sem("o_store")
        scattered = sem("scattered")
        consts, may_add = sem("consts"), sem("may_add")
        pool_order, dve_order, act_order = sem("pool_order"), sem("dve_order"), sem("act_order")
        keys, key_tr, keyc_done, idx_ready = sem("keys"), sem("key_tr"), sem("keyc_done"), sem("idx_ready")
        eq_done = sem("eq_done")
        st_done, var_ready, sd_ready, xn_done = sem("st_done"), sem("var_ready"), sem("sd_ready"), sem("xn_done")
        tr_done, xt_hi, xt_lo = sem("tr_done"), sem("xt_hi"), sem("xt_lo")
        w_hi, w_lo = sem("w_hi"), sem("w_lo")
        v_mm, v_hi, v_lo = sem("v_mm"), sem("v_hi"), sem("v_lo")

        features, pair_weights, node_work = ExitStack(), ExitStack(), ExitStack()
        XH, XL = right(features, [("XH", [P, KT, N], F32R), ("XL", [P, KT, N], F32R)])
        ws, wqkH, wqkL = right(pair_weights, [("ws", [P, 2, KT, P], F32), ("wqkH", [P, 2, KT, P], F32R),
                                              ("wqkL", [P, 2, KT, P], F32R)])
        (xn, zeros, ekeys, key_t, kb, wst, wH, wL, VS, brow, triw, keyc, etmp) = region([
            ("xn", [T, NT, D], F32), ("zeros", [T, N], F32),
            ("ekeys", [EROWS, 2, 250], I32), ("key_t", [EROWS, 250], F32),
            ("kb", [T, 2, EC, T], F32), ("wst", [P, 2, 2, D], F32),
            ("wH", [P, KT, D], F32R), ("wL", [P, KT, D], F32R),
            ("VS", [T, 2, H, 2, HD], F32R), ("brow", [3 * PAIRS, P], F32),
            ("triw", [T, T], F32),
            ("keyc", [T, ET], F32), ("etmp", [T, 3, EC], F32)])

        CK = [("K32", [P, N], F32), ("Q32", [P, N], F32), ("OUN", [P, N], F32), ("R32", [P, N], F32),
              ("rden", [P, N], F32), ("kt2", [T, NT, 2, P], F32R), ("vsb", [T, NT, 4 * HD], F32R),
              ("OHL", [P, 2, N], F32R), ("tmpo", [HD, 2, CW], F32),
              ("Pf", [T, RING, 2, CW], F32), ("Ph", [T, RING, 2, CW], F32R), ("Pl", [T, RING, 2, CW], F32R),
              ("gs", [P, 3, P], F32), ("k1", [P, 4], F32)]
        (K32, Q32, OUN, R32, rden, kt2, vsb, OHL, tmpo, Pf, Ph, Pl, gs, k1, KHA, KHB, KLA, KLB, MA, MB) = region(
            CK + [(n, [P, N], F32R) for n in ("KHA", "KHB", "KLA", "KLB", "MA", "MB")])
        KH, KL, MQ = (KHA, KHB), (KLA, KLB), (MA, MB)
        wqk_in, v_in = sem("wqk_in"), sem("v_in")
        wqk_hi, wqk_lo, bias_ready = sem("wqk_hi"), sem("wqk_lo"), sem("bias_ready")
        qk_mm, qk_evac, kq_hi, kq_lo, k1_done = (sem("qk_mm"), sem("qk_evac"), sem("kq_hi"), sem("kq_lo"),
                                                 sem("k1_done"))
        sc_done, sq_done, p_hiA, p_hiD, p_lo, pv_done, acc_done = (
            sem("sc_done"), sem("sq_done"), sem("p_hiA"), sem("p_hiD"), sem("p_lo"), sem("pv_done"), sem("acc_done"))
        tmp_done, oacc_done = sem("tmp_done"), sem("oacc_done")
        kt_mm, kt_hi, kt_lo, g_mm, gfin_done = sem("kt_mm"), sem("kt_hi"), sem("kt_lo"), sem("g_mm"), sem("gfin_done")
        gq_mm, r_done, den_mm, rden_done = sem("gq_mm"), sem("r_done"), sem("den_mm"), sem("rden_done")
        o_fin, ohl_free, pair_order = sem("o_fin"), sem("ohl_free"), sem("pair_order")

        pair_weights.close()
        third = ExitStack()
        bgp, wst3, wH3, wL3, HH, HL, Cs = left(third, [
            ("bgp", [T, D], F32), ("wst3", [P, 2, 2, D], F32), ("wH3", [P, KT, D], F32R), ("wL3", [P, KT, D], F32R),
            ("HH", [T, NT, D], F32R), ("HL", [T, NT, D], F32R), ("Cs", [T, 2, NT, T], F32)])
        features.close()
        XF, = right(ctx, [("XF", [T, NT, D], F32)])
        Csc, CH, CL, oS, xr, t0_, xfT = right(node_work, [
            ("Csc", [T, NT, T], F32), ("CH", [T, 2, NT, T], F32R), ("CL", [T, 2, NT, T], F32R),
            ("oS", [P, PAIRS, 2, T], F32R), ("xr", [T, 2, D], F32), ("t0_", [T, 2, D], F32),
            ("xfT", [P, KT, T], F32)])
        third.close()
        node_work.close()
        h_mm, h_hi, h_lo, deg_mm, dinv_sd, dinv_done = (sem("h_mm"), sem("h_hi"), sem("h_lo"), sem("deg_mm"),
                                                        sem("dinv_sd"), sem("dinv_done"))
        cs_in, xr_in = [sem("cs_in0"), sem("cs_in1")], [sem("xr_in0"), sem("xr_in1")]
        os_in, bias_in, x1_store = sem("os_in"), sem("bias_in"), [sem("x1_store0"), sem("x1_store1")]
        csc_done, ch_done, cl_done = sem("csc_done"), sem("ch_done"), sem("cl_done")
        pj_mm, pj_read, agg_mm, x1_done = sem("pj_mm"), sem("pj_read"), sem("agg_mm"), sem("x1_done")
        var2, sd2, xf_done, xf_tr, xf_evac, lg_mm, lg_done = (sem("var2"), sem("sd2"), sem("xf_done"), sem("xf_tr"),
                                                              sem("xf_evac"), sem("lg_mm"), sem("lg_done"))
        (w1s, w2s, w1H, w1L, w2H, w2L, xe, xeH, xeL, h32, hH, hL, oE, b2r, Bt, PM, b1row, same) = region([
            ("w1s", [P, KT, F], F32), ("w2s", [P, FT, D], F32),
            ("w1H", [P, 2, KT, F], F32R), ("w1L", [P, 2, KT, F], F32R),
            ("w2H", [P, 2, FT, D], F32R), ("w2L", [P, 2, FT, D], F32R),
            ("xe", [98, 2, 2, D], F32), ("xeH", [P, KT, CAPP], F32R), ("xeL", [P, KT, CAPP], F32R),
            ("h32", [P, FT, CAPP], F32), ("hH", [P, FT, CAPP], F32R), ("hL", [P, FT, CAPP], F32R),
            ("oE", [98, 2, D], F32), ("b2r", [98, 2, D], F32), ("Bt", [T, NT, N], BF16), ("PM", [T, N], F32),
            ("b1row", [E * FT, P], F32), ("same", [T, 2, T], F32)])
        ex_done, pm_done, pm_mm, pm_evac, b_done, cnt_mm, slot_done = (
            sem("ex_done"), sem("pm_done"), sem("pm_mm"), sem("pm_evac"), sem("b_done"), sem("cnt_mm"), sem("slot_done"))
        dm_done, route_order = sem("dm_done"), sem("route_order")
        sent = sem("sent")
        b1_in, b1_tr, b1_done, b1cur_done = sem("b1_in"), sem("b1_tr"), sem("b1_done"), sem("b1cur_done")
        we_in, we_hi, we_lo = sem("we_in"), sem("we_hi"), sem("we_lo")
        xe_in, b2_in = [sem("xe_in0"), sem("xe_in1")], [sem("b2_in0"), sem("b2_in1")]
        xe_tr, xe_hi, xe_lo, m1_mm, h_act, hh_done, hl_done, m2_mm, oe_done, oe_store = (
            sem("xe_tr"), sem("xe_hi"), sem("xe_lo"), sem("m1_mm"), sem("h_act"), sem("hh_done"), sem("hl_done"),
            sem("m2_mm"), sem("oe_done"), sem("oe_store"))
        pads, same_done, we_lo1, oe_free = sem("pads"), sem("same_done"), sem("we_lo1"), sem("oe_free")
        yg, = region([("yg", [T, NT, D], F32)])
        got = [sem(f"got{i}") for i in range(NT)]
        x1_back, out_done, stored = sem("x1_back"), sem("out_done"), sem("stored")

        block = ctx.enter_context(nc.Block())

        w_parts = [(w_qkv[:, 2 * D:3 * D], 0), (gnn_w, 1), (w_proj, 2)]
        GROUPS = [(0, 4), (4, 4), (8, 2)]

        @block.sync
        def _(sp):
            for i in range(NT):
                sp.dma_start(xn[:, i, :], x[i * T:(i + 1) * T, :]).then_inc(x_in[i], 16)
                if i == 1:
                    sp.dma_start(ekeys[:, 0, :], src.rearrange("(p n) -> p n", p=EROWS)).then_inc(e_in, 16)
                    sp.dma_start(ekeys[:, 1, :], dst.rearrange("(p n) -> p n", p=EROWS)).then_inc(e_in, 16)

            def load_w(wc):
                w = w_parts[wc // 3][0]
                k = 2 * (wc % 3)
                if wc >= 2:
                    sp.wait_ge(w_lo, wc - 1)
                sp.dma_start(wst[:, wc % 2, :, :],
                             w[k * P:(k + 2) * P, :].rearrange("(k p) n -> p k n", p=P)).then_inc(w_in[wc % 2], 16)

            load_w(0)
            load_w(1)
            sp.dma_start(brow[:], b_qkv.rearrange("(c p) -> c p", p=P)).then_inc(b_in, 16)
            sp.wait_ge(keys, 1)
            sp.dma_start(keyd, key_t[:]).then_inc(key_out, 16)
            load_w(2)
            sp.wait_ge(key_out, 16)

            def load_keys(u):
                if u >= 2:
                    sp.wait_ge(eq_done, u - 1)
                half, r0 = u // 5, (u % 5) * EC
                rows_of = keyd[r0:r0 + EC, half * T:(half + 1) * T]
                sp.dma_start(kb[:, u % 2, :, :], rows_of.unsqueeze(0).broadcast_to([T, EC, T])
                             ).then_inc(kb_in[u % 2], 16)

            load_keys(0)
            load_keys(1)
            for i in range(NT):
                sp.wait_ge(v_lo, 2 * i + 2)
                sp.dma_start(vdram[:, i, :].rearrange("(j p) f -> p j f", p=T),
                             VS[:, i % 2].bitcast(F32).rearrange("p (j a) l f -> p j (a l f)", a=2)
                             ).then_inc(v_store[i % 2], 16)
                if i + 2 < EU:
                    load_keys(i + 2)

        @block.gpsimd
        def _(pool):
            order = Chain(pool, pool_order)
            order(pool.memset(zeros[:], 0.0))
            pool.dma_start(counts[0:N * N, :].rearrange("(s p d) o -> p s (d o)", p=T, d=N),
                           zeros[:].unsqueeze(1).broadcast_to([T, NT, N])).then_inc(scattered, 16)
            pool.dma_start(counts[N * N:N * N + T, :].rearrange("(a d) o -> a (d o)", a=1),
                           zeros[0:1, 0:T]).then_inc(scattered, 16)
            pool.dma_start(rows[0:SLOTS, :].rearrange("(p s) d -> p s d", p=120),
                           zeros[0:120, 0:D].unsqueeze(1).broadcast_to([120, 13, D])).then_inc(r_zero, 16)
            pool.dma_start(rows[SLOTS:, :].rearrange("(p s) d -> p s d", p=T),
                           zeros[:, 0:D].unsqueeze(1).broadcast_to([T, NT, D])).then_inc(r_zero, 16)
            order(pool.memset(ident[:], 0.0))
            order(pool.affine_select(out=ident[:], in_=ident[:], compare_op=ALU.not_equal, fill=1.0, base=0,
                                     pattern=[[-1, P]], channel_multiplier=1))
            order(pool.memset(triw[:], 1.0))
            order(pool.affine_select(out=triw[:], in_=triw[:], compare_op=ALU.is_ge, fill=1.0 + AGAIN, base=0,
                                     pattern=[[1, T]], channel_multiplier=-1))
            order(pool.memset(later[:], 1.0))
            order(pool.affine_select(out=later[:], in_=later[:], compare_op=ALU.is_gt, fill=0.0, base=0,
                                     pattern=[[1, T]], channel_multiplier=-1))
            order(pool.memset(blocks[:], 0.0))
            order(pool.memset(blocks[0:HD, 0:HD], 1.0))
            order(pool.memset(blocks[HD:P, HD:P], 1.0))
            order(pool.memset(ones2[:], 1.0))
            order(pool.iota(iota_i[:, 0:16], pattern=[[T, 16]], base=0, channel_multiplier=1))
            order(pool.iota(iota_i[:, 10:11], pattern=[[0, 1]], base=N * N, channel_multiplier=1))
            order(pool.iota(iota_i[:, 16:32], pattern=[[1, 16]], base=0, channel_multiplier=0))
            pool.tensor_copy(iota_f[:], iota_i[:]).then_inc(consts, 1)
            pool.wait_ge(consts, 1)
            base = order.n
            with pool.Fori(0, EU) as u:
                pool.wait_ge(idx_ready, u + 1)
                for s in range(EC):
                    done = u * (2 * EC) + (base + 2 * s)
                    pool.tensor_copy(icur[:, s % 2:s % 2 + 1], idxf[:, at(u * EC + s, 1)]).then_inc(pool_order, 1)
                    pool.tensor_copy(vcur[:, s % 2:s % 2 + 1], countc[:, at(u * EC + s, 1)]).then_inc(pool_order, 1)
                    pool.wait_ge(pool_order, done + 2)
                    pool.wait_ge(scattered, u * (16 * EC) + (CLEARED + 16 * s))
                    pool.sem_inc(may_add, 1)
                    pool.indirect_dma_start(
                        out=counts, out_offset=bass.IndirectOffsetOnAxis(ap=icur[:, s % 2:s % 2 + 1], axis=0),
                        in_=vcur[:, s % 2:s % 2 + 1], in_offset=None, compute_op=ALU.add).then_inc(scattered, 16)
            pool.wait_ge(scattered, CLEARED + 16 * ET)

        @block.scalar
        def _(act):
            act.wait_ge(var_ready, 1)
            act.activation(rs[:, 1, :], rs[:, 0, :], ACT.Sqrt).then_inc(sd_ready, 1)

            def split_w(wc):
                act.wait_ge(w_in[wc % 2], 16 * (wc // 2 + 1))
                act.activation(wH[:, 2 * (wc % 3):2 * (wc % 3) + 2, :], wst[:, wc % 2, :, :], ACT.Copy).then_inc(w_hi, 1)

            for wc in range(3):
                split_w(wc)
            g = 0
            for t0, nt in GROUPS:
                for k in range(KT):
                    act.wait_ge(tr_done, g + 1)
                    act.activation(XH[:, k, t0 * T:(t0 + nt) * T], ps[:, g % 4, 0:nt * T], ACT.Copy).then_inc(xt_hi, 1)
                    g += 1
            for vg in range(2 * NT):
                i, c = vg // 2, vg % 2
                act.wait_ge(v_mm, vg + 1)
                if i >= 2:
                    act.wait_ge(v_store[i % 2], 16 * (i // 2))
                act.activation(VS[:, i % 2, 6 * c:6 * c + 6, 0, :],
                               ps[0:T, 4 + vg % 4, 0:HALF].rearrange("p (h f) -> p h f", h=6), ACT.Copy).then_inc(v_hi, 1)

        @block.vector
        def _(dve):
            order = Chain(dve, dve_order)
            dve.wait_ge(e_in, 32)
            dve.scalar_tensor_tensor(out=key_t[:], in0=ekeys[:, 0, :], scalar=float(N), in1=ekeys[:, 1, :],
                                     op0=ALU.mult, op1=ALU.add).then_inc(keys, 1)
            for i in range(NT):
                dve.wait_ge(x_in[i], 16)
                for c in range(2):
                    dve.bn_stats(stats[:, i, c, :], xn[:, i, c * HALF:(c + 1) * HALF]).then_inc(st_done, 1)
                if i >= 1:
                    dve.wait_ge(st_done, 2 * i)
                    dve.bn_aggr(mv[:, i - 1, :], stats[:, i - 1])
            dve.wait_ge(st_done, 2 * NT)
            order(dve.bn_aggr(mv[:, NT - 1, :], stats[:, NT - 1]))
            dve.tensor_scalar(rs[:, 0, :], mv[:, :, 1], EPS, None, ALU.add).then_inc(var_ready, 1)
            dve.wait_ge(var_ready, 1)
            dve.wait_ge(sd_ready, 1)
            order(dve.reciprocal(rs[:, 2, :], rs[:, 1, :]))
            order(dve.tensor_tensor(rs[:, 3, :], rs[:, 2, :], rs[:, 2, :], ALU.mult))
            order(dve.tensor_tensor(rs[:, 3, :], rs[:, 3, :], rs[:, 0, :], ALU.mult))
            order(dve.tensor_scalar(rs[:, 3, :], rs[:, 3, :], -0.5, 1.5, ALU.mult, ALU.add))
            order(dve.tensor_tensor(rs[:, 3, :], rs[:, 3, :], rs[:, 2, :], ALU.mult))
            for i in range(NT):
                dve.tensor_scalar(xn[:, i, :], xn[:, i, :], mv[:, i, 0:1], rs[:, 3, i:i + 1],
                                  ALU.subtract, ALU.mult).then_inc(xn_done, 1)

            def split_w(wc):
                dve.wait_ge(w_hi, wc + 1)
                k = 2 * (wc % 3)
                dve.tensor_tensor(wL[:, k:k + 2, :], wst[:, wc % 2, :, :], wH[:, k:k + 2, :].bitcast(F32),
                                  ALU.subtract).then_inc(w_lo, 1)

            def edge_chunk(u):
                dve.wait_ge(kb_in[u % 2], 16 * (u // 2 + 1))
                for s in range(EC):
                    c = u * EC + s
                    ins = dve.scalar_tensor_tensor(out=kb[:, u % 2, s, :], in0=kb[:, u % 2, s, :],
                                                   scalar=keyc[:, c:c + 1], in1=triw[:], op0=ALU.is_equal,
                                                   op1=ALU.mult, accum_out=countc[:, c:c + 1])
                order(ins)
                cs = slice(u * EC, (u + 1) * EC)
                order(dve.tensor_scalar(etmp[:, 0, :], countc[:, cs], AGAIN, None, ALU.is_ge))
                order(dve.tensor_scalar(etmp[:, 1, :], keyc[:, cs], -1.0, iota_f[:, 10:11], ALU.mult, ALU.add))
                order(dve.tensor_tensor(etmp[:, 2, :], etmp[:, 0, :], etmp[:, 1, :], ALU.mult))
                ins = dve.tensor_tensor(idxf[:, cs], etmp[:, 2, :], keyc[:, cs], ALU.add)
                ins.then_inc(idx_ready, 1)
                dve.wait_ge(idx_ready, u + 1)
                dve.sem_inc(eq_done, 1)

            for wc in range(2):
                split_w(wc)
            g = 0
            for t0, nt in GROUPS:
                for k in range(KT):
                    dve.wait_ge(xt_hi, g + 1)
                    dve.tensor_tensor(XL[:, k, t0 * T:(t0 + nt) * T], ps[:, g % 4, 0:nt * T],
                                      XH[:, k, t0 * T:(t0 + nt) * T].bitcast(F32), ALU.subtract).then_inc(xt_lo, 1)
                    g += 1
                if t0 == 0:
                    dve.wait_ge(key_tr, 1)
                    order(dve.memset(bcols[:, :, PAIRS:], 0.0))
                    bias = ps[:, 7, ET:ET + 3 * PAIRS].rearrange("p (s j) -> p s j", s=3)
                    dve.tensor_copy(bcols[:, 1:3, 0:PAIRS], bias[:, 1:3, :]).then_inc(keyc_done, 1)
                    dve.tensor_scalar(bcols[:, 0, 0:PAIRS], bias[:, 0, :], SCALE, None, ALU.mult).then_inc(keyc_done, 1)
                    dve.tensor_copy(keyc[:], ps[0:T, 7, 0:ET]).then_inc(keyc_done, 1)
                    dve.wait_ge(keyc_done, 3)
                    dve.wait_ge(consts, 1)
                    split_w(2)
                    edge_chunk(0)
            for vg in range(2 * NT):
                i, c = vg // 2, vg % 2
                dve.wait_ge(v_hi, vg + 1)
                dve.tensor_tensor(VS[:, i % 2, 6 * c:6 * c + 6, 1, :],
                                  ps[0:T, 4 + vg % 4, 0:HALF].rearrange("p (h f) -> p h f", h=6),
                                  VS[:, i % 2, 6 * c:6 * c + 6, 0, :].bitcast(F32), ALU.subtract).then_inc(v_lo, 1)
                if vg % 2 == 1 and vg // 2 < EU - 1:
                    edge_chunk(1 + vg // 2)

        @block.tensor
        def _(pe):
            pe.wait_ge(consts, 1)
            g = 0
            for t0, nt in GROUPS:
                pe.wait_ge(xn_done, t0 + nt)
                for k in range(KT):
                    if g >= 4:
                        pe.wait_ge(xt_lo, g - 3)
                    for t in range(nt):
                        ins = pe.transpose(ps[:, g % 4, t * T:(t + 1) * T], xn[:, t0 + t, k * P:(k + 1) * P],
                                           ident[0:T, 0:T])
                    ins.then_inc(tr_done, 1)
                    g += 1
                if t0 == 0:
                    pe.wait_ge(keys, 1)
                    for half in range(2):
                        ins = pe.transpose(ps[0:T, 7, half * EROWS:(half + 1) * EROWS],
                                           key_t[:, half * T:(half + 1) * T], ident[0:EROWS, 0:EROWS])
                    pe.wait_ge(b_in, 16)
                    ins = pe.transpose(ps[:, 7, 2 * EROWS:2 * EROWS + 3 * PAIRS], brow[:], ident[0:3 * PAIRS, 0:3 * PAIRS])
                    ins.then_inc(key_tr, 1)
            pe.wait_ge(keyc_done, 3)
            for vg in range(2 * NT):
                i, c = vg // 2, vg % 2
                if vg == 0:
                    pe.wait_ge(w_lo, 3)
                    pe.wait_ge(xt_lo, 3 * KT)
                if vg >= 4:
                    pe.wait_ge(v_lo, vg - 3)
                ins = product(pe, ps[0:T, 4 + vg % 4, 0:HALF],
                              lambda k: (XH[:, k, i * T:(i + 1) * T], XL[:, k, i * T:(i + 1) * T]),
                              lambda k: (wH[:, k, c * HALF:(c + 1) * HALF], wL[:, k, c * HALF:(c + 1) * HALF]), KT)
                ins.then_inc(v_mm, 1)

        HI_ON_ACT = [i % 5 in (1, 3) for i in range(STEPS)]
        NA = sum(HI_ON_ACT)
        ND = STEPS - NA
        FREE = 1

        def step(i):
            a, c, kp = i // 15, (i // 5) % 3, i % 5
            return a, c, kp, CHUNKS[c][0], CHUNKS[c][1]

        def values_over(eng):
            eng.wait_ge(v_store[0], 80)
            eng.wait_ge(v_store[1], 80)
            eng.wait_ge(v_mm, 2 * NT)
            eng.wait_ge(idx_ready, EU)
            eng.wait_ge(scattered, CLEARED)
            eng.wait_ge(r_zero, 32)

        @block.sync
        def _(sp):
            def load_wqk(j):
                for s_ in range(2):
                    sp.dma_start(ws[:, s_], w_qkv[:, at(j * P + s_ * D, P)].rearrange("(k p) n -> p k n", p=P)
                                 ).then_inc(wqk_in, 16)

            def load_v(j):
                sp.dma_start(vsb[:].bitcast(F32), vdram[at(j * T, T)]).then_inc(v_in, 16)

            def store_o(j):
                sp.wait_ge(o_fin, 3 * j + 3)
                for l in range(2):
                    sp.dma_start(odram[at(j * P, P), :, l, :],
                                 OHL[:, l, :].bitcast(F32).rearrange("p (i t) -> p i t", t=T)).then_inc(o_store, 16)
                sp.wait_ge(o_store, 32 * j + 32)
                sp.sem_inc(ohl_free, 1)

            load_wqk(0)
            sp.sem_inc(ohl_free, FREE)
            values_over(sp)
            load_v(0)
            with sp.Fori(0, PAIRS - 1) as j:
                sp.wait_ge(wqk_lo, j + 1)
                load_wqk(j + 1)
                sp.wait_ge(pv_done, j * STEPS + STEPS)
                load_v(j + 1)
                store_o(j)
            sp.wait_ge(wqk_lo, PAIRS)
            load_wqk(PAIRS)
            store_o(PAIRS - 1)

        @block.scalar
        def _(act):
            def split_wqk(j):
                act.wait_ge(wqk_in, 32 * j + 32)
                act.activation(wqkH[:], ws[:], ACT.Copy).then_inc(wqk_hi, 1)

            split_wqk(0)
            values_over(act)
            with act.Fori(0, PAIRS) as j:
                act.wait_ge(rden_done, 3 * j + FREE)
                act.wait_ge(bias_ready, j + 1)
                for g in range(6):
                    s_, c = (1, g) if g < 3 else (0, g - 3)
                    c0, w = CHUNKS[c]
                    bank = ps[:, (6, 7, 4, 5, 6, 7)[g], 0:w]
                    act.wait_ge(qk_mm, 6 * j + (g + 1))
                    if s_ == 1:
                        act.activation(K32[:, c0:c0 + w], bank, ACT.Identity, bias=pbias[:, 1:2],
                                       accum_out=k1[:, c:c + 1]).then_inc(qk_evac, 1)
                        act.wait_ge(qk_evac, 6 * j + (g + 1))
                        for a in range(2):
                            for half in range(2):
                                ins = act.activation(KH[a][half * HD:(half + 1) * HD, c0:c0 + w],
                                                     K32[a * HD:(a + 1) * HD, c0:c0 + w], ACT.Copy)
                    else:
                        act.activation(Q32[:, c0:c0 + w], bank, ACT.Identity, bias=pbias[:, 0:1],
                                       scale=SCALE).then_inc(qk_evac, 1)
                        act.wait_ge(qk_evac, 6 * j + (g + 1))
                        for a in range(2):
                            h = slice(a * HD, (a + 1) * HD)
                            ins = act.activation(MQ[a][h, c0:c0 + w], Q32[h, c0:c0 + w], ACT.Copy)
                    ins.then_inc(kq_hi, 1)

                def round_weights(i):
                    w = step(i)[4]
                    act.wait_ge(sq_done, j * STEPS + (i + 1))
                    if i >= RING:
                        act.wait_ge(pv_done, j * STEPS + (i - RING + 1))
                    act.activation(Ph[:, i % RING, :, 0:w], Pf[:, i % RING, :, 0:w], ACT.Identity,
                                   bias=1.0).then_inc(p_hiA, 1)

                def fold_out(s):
                    w = CHUNKS[s % 3][1]
                    act.wait_ge(acc_done, 6 * j + (s + 1))
                    if s >= 2:
                        act.wait_ge(oacc_done, 6 * j + (s - 1 + FREE))
                    act.activation(tmpo[:, s % 2, 0:w], ps[HD:P, 4 + s % 2, 0:w], ACT.Copy).then_inc(tmp_done, 1)

                def turn_k(n):
                    t0, nt = GROUPS[n]
                    act.wait_ge(kt_mm, 3 * j + (n + 1))
                    act.activation(kt2[:, t0:t0 + nt, 0, :],
                                   ps[0:T, 6 + n % 2, 0:nt * P].rearrange("p (t f) -> p t f", f=P),
                                   ACT.Copy).then_inc(kt_hi, 1)

                for i in range(STEPS):
                    w = step(i)[4]
                    act.wait_ge(sc_done, j * STEPS + (i + 1))
                    if i >= RING:
                        act.wait_ge(p_lo, j * STEPS + (i - RING + 1))
                    act.activation(Pf[:, i % RING, :, 0:w], ps[0:T, 2 * (i % 2):2 * (i % 2) + 2, 0:w], ACT.Square,
                                   bias=1.0).then_inc(sq_done, 1)
                    if i >= 1 and HI_ON_ACT[i - 1]:
                        round_weights(i - 1)
                    if i in (3, 4, 6):
                        turn_k((3, 4, 6).index(i))
                    if i % 5 == 3 and i >= 8:
                        fold_out(i // 5 - 1)
                    if i == 10:
                        split_wqk(j + 1)
                if HI_ON_ACT[STEPS - 1]:
                    round_weights(STEPS - 1)
                fold_out(5)

        @block.vector
        def _(dve):
            def split_wqk(j):
                dve.wait_ge(wqk_hi, j + 1)
                dve.tensor_tensor(wqkL[:], ws[:], wqkH[:].bitcast(F32), ALU.subtract).then_inc(wqk_lo, 1)

            def pair_bias(j):
                dve.tensor_scalar(pbias[:], bcols[:, 0:2, at(j, 1)].rearrange("p s o -> p (s o)"), 1.0, None,
                                  ALU.mult).then_inc(bias_ready, 1)

            split_wqk(0)
            pair_bias(0)
            dve.sem_inc(rden_done, FREE)
            dve.sem_inc(oacc_done, FREE)
            values_over(dve)
            PER_PAIR = 13
            with dve.Fori(0, PAIRS) as j:
                order = Chain(dve, pair_order, j * PER_PAIR)
                for g in range(6):
                    c0, w = CHUNKS[g % 3]
                    cs = slice(c0, c0 + w)
                    dve.wait_ge(kq_hi, 6 * j + (g + 1))
                    for a in range(2):
                        own, other = slice(a * HD, (a + 1) * HD), slice((1 - a) * HD, (2 - a) * HD)
                        if g < 3:
                            for half in (own, other):
                                ins = dve.tensor_tensor(KL[a][half, cs], K32[own, cs], KH[a][own, cs].bitcast(F32),
                                                        ALU.subtract)
                        else:
                            ins = dve.tensor_tensor(MQ[a][other, cs], Q32[own, cs], MQ[a][own, cs].bitcast(F32),
                                                    ALU.subtract)
                    ins.then_inc(kq_lo, 1)
                    if g == 2:
                        order(dve.tensor_reduce(k1[:, 3:4], k1[:, 0:3], AX.X, ALU.add))
                        order(dve.tensor_scalar(k1[:, 3:4], k1[:, 3:4], 2.0, None, ALU.mult))

                def gram():
                    dve.wait_ge(g_mm, j + 1)
                    order(dve.tensor_scalar(gs[:, 0, :], ps[:, 7, P:2 * P], 2.0, None, ALU.mult))
                    order(dve.tensor_tensor(gs[:, 1, :], ps[:, 7, 0:P], gs[:, 0, :], ALU.add))
                    dve.tensor_tensor(gs[:, 2, :], gs[:, 1, :], blocks[:], ALU.mult).then_inc(gfin_done, 1)

                def turn_k(n):
                    t0, nt = GROUPS[n]
                    dve.wait_ge(kt_hi, 3 * j + (n + 1))
                    dve.tensor_tensor(kt2[:, t0:t0 + nt, 1, :],
                                      ps[0:T, 6 + n % 2, 0:nt * P].rearrange("p (t f) -> p t f", f=P),
                                      kt2[:, t0:t0 + nt, 0, :].bitcast(F32), ALU.subtract).then_inc(kt_lo, 1)

                def quadratic(c):
                    c0, w = CHUNKS[c]
                    dve.wait_ge(gq_mm, 3 * j + (c + 1))
                    dve.scalar_tensor_tensor(out=R32[:, c0:c0 + w], in0=ps[:, 6 + c % 2, 0:w], scalar=k1[:, 3:4],
                                             in1=Q32[:, c0:c0 + w], op0=ALU.add, op1=ALU.mult).then_inc(r_done, 1)

                def total(c):
                    c0, w = CHUNKS[c]
                    dve.wait_ge(den_mm, 3 * j + (c + 1))
                    order(dve.tensor_scalar(rden[:, c0:c0 + w], ps[:, 7 - c % 2, 0:w], 2.0 * N, None, ALU.add))
                    dve.reciprocal(rden[:, c0:c0 + w], rden[:, c0:c0 + w]).then_inc(rden_done, 1)

                def fold_out(s):
                    a, (c0, w) = s // 3, CHUNKS[s % 3]
                    dve.wait_ge(tmp_done, 6 * j + (s + 1))
                    dve.tensor_tensor(OUN[a * HD:(a + 1) * HD, c0:c0 + w], ps[0:HD, 4 + s % 2, 0:w],
                                      tmpo[:, s % 2, 0:w], ALU.add).then_inc(oacc_done, 1)

                def finish(c):
                    c0, w = CHUNKS[c]
                    cs = slice(c0, c0 + w)
                    bv = bcols[:, 2, at(j, 1)]
                    dve.wait_ge(oacc_done, 6 * j + (4 + c + FREE))
                    dve.wait_ge(rden_done, 3 * j + (c + 1 + FREE))
                    order(dve.tensor_tensor(R32[:, cs], OUN[:, cs], rden[:, cs], ALU.mult))
                    if c == 0:
                        dve.wait_ge(ohl_free, j + FREE)
                    order(dve.tensor_scalar(OHL[:, 0, cs], R32[:, cs], bv, None, ALU.add))
                    ins = dve.scalar_tensor_tensor(out=OHL[:, 1, cs], in0=R32[:, cs], scalar=bv,
                                                   in1=OHL[:, 0, cs].bitcast(F32), op0=ALU.add, op1=ALU.subtract)
                    ins.then_inc(o_fin, 1)
                    dve.wait_ge(o_fin, 3 * j + (c + 1))

                for i in range(STEPS):
                    w = step(i)[4]
                    p, f, h = Pl[:, i % RING, :, 0:w], Pf[:, i % RING, :, 0:w], Ph[:, i % RING, :, 0:w]
                    if i >= RING:
                        dve.wait_ge(pv_done, j * STEPS + (i - RING + 1))
                    if HI_ON_ACT[i]:
                        dve.wait_ge(p_hiA, j * NA + (sum(HI_ON_ACT[:i]) + 1))
                    else:
                        dve.wait_ge(sq_done, j * STEPS + (i + 1))
                        dve.tensor_scalar(h, f, 1.0, None, ALU.add).then_inc(p_hiD, 1)
                        dve.wait_ge(p_hiD, j * ND + (i - sum(HI_ON_ACT[:i]) + 1))
                    dve.scalar_tensor_tensor(out=p, in0=f, scalar=1.0, in1=h.bitcast(F32), op0=ALU.add,
                                             op1=ALU.subtract).then_inc(p_lo, 1)
                    if i in (4, 5, 7):
                        turn_k((4, 5, 7).index(i))
                    if i == 9:
                        gram()
                    if i == 12:
                        split_wqk(j + 1)
                        pair_bias(j + 1)
                    if i in (14, 15, 17):
                        quadratic((14, 15, 17).index(i))
                    if i in (20, 21, 23):
                        total((20, 21, 23).index(i))
                    if i % 5 == 4 and i >= 9:
                        fold_out(i // 5 - 1)
                    if i == 26:
                        finish(0)
                fold_out(5)
                finish(1)
                finish(2)
                assert order.n == PER_PAIR, order.n

        @block.tensor
        def _(pe):
            values_over(pe)
            with pe.Fori(0, PAIRS) as j:
                pe.wait_ge(wqk_lo, j + 1)
                pe.wait_ge(rden_done, 3 * j + FREE)
                pe.wait_ge(oacc_done, 6 * j + FREE)
                for g in range(6):
                    s_, c = (1, g) if g < 3 else (0, g - 3)
                    c0, w = CHUNKS[c]
                    if g >= 4:
                        pe.wait_ge(qk_evac, 6 * j + (g - 3))
                    product(pe, ps[:, (6, 7, 4, 5, 6, 7)[g], 0:w],
                            lambda k: (wqkH[:, s_, k, :], wqkL[:, s_, k, :]),
                            lambda k: (XH[:, k, c0:c0 + w], XL[:, k, c0:c0 + w]), KT).then_inc(qk_mm, 1)

                def turn_k(n):
                    t0, nt = GROUPS[n]
                    if n == 0:
                        pe.wait_ge(qk_evac, 6 * j + 6)
                    if n == 2:
                        pe.wait_ge(kt_lo, 3 * j + 1)
                    for t in range(nt):
                        ins = pe.transpose(ps[0:T, 6 + n % 2, t * P:(t + 1) * P],
                                           K32[:, (t0 + t) * T:(t0 + t + 1) * T], ident[:])
                    ins.then_inc(kt_mm, 1)

                def gram():
                    pe.wait_ge(kt_lo, 3 * j + 3)
                    for t in range(NT):
                        ins = pe.matmul(ps[:, 7, 0:2 * P], kt2[:, t, 0, :], kt2[:, t].rearrange("p l f -> p (l f)"),
                                        start=(t == 0), stop=(t == NT - 1))
                    ins.then_inc(g_mm, 1)

                def quadratic(c):
                    c0, w = CHUNKS[c]
                    pe.wait_ge(gfin_done, j + 1)
                    if c == 2:
                        pe.wait_ge(r_done, 3 * j + 1)
                    pe.matmul(ps[:, 6 + c % 2, 0:w], gs[:, 2, :], Q32[:, c0:c0 + w], start=True,
                              stop=True).then_inc(gq_mm, 1)

                def total(c):
                    c0, w = CHUNKS[c]
                    pe.wait_ge(r_done, 3 * j + min(c + 2, 3))
                    if c == 2:
                        pe.wait_ge(rden_done, 3 * j + (1 + FREE))
                    pe.matmul(ps[:, 7 - c % 2, 0:w], blocks[:], R32[:, c0:c0 + w], start=True,
                              stop=True).then_inc(den_mm, 1)

                for i in range(STEPS + LAG):
                    if i < STEPS:
                        a, c, kp, c0, w = step(i)
                        if i % 5 == 0 and a == 0:
                            pe.wait_ge(kq_lo, 6 * j + (4 + c))
                        if i >= 2:
                            pe.wait_ge(sq_done, j * STEPS + (i - 1))
                        for t in range(2):
                            kt = 2 * kp + t
                            out_ = ps[0:T, 2 * (i % 2) + t, 0:w]
                            q = MQ[a][:, c0:c0 + w]
                            pe.matmul(out_, KH[a][:, kt * T:(kt + 1) * T], q, start=True, stop=False)
                            ins = pe.matmul(out_, KL[a][:, kt * T:(kt + 1) * T], q, start=False, stop=True)
                        ins.then_inc(sc_done, 1)
                    if i >= LAG:
                        m = i - LAG
                        a, c, kp, c0, w = step(m)
                        s = m // 5
                        if m == 0:
                            pe.wait_ge(v_in, 16 * j + 16)
                        if m % 5 == 0 and s >= 2:
                            pe.wait_ge(oacc_done, 6 * j + (s - 1 + FREE))
                        pe.wait_ge(p_lo, j * STEPS + (m + 1))
                        for t in range(2):
                            for part in (Ph, Pl):
                                ins = pe.matmul(ps[:, 4 + s % 2, 0:w], vsb[:, 2 * kp + t, a * P:(a + 1) * P],
                                                part[:, m % RING, t, 0:w], start=(kp == 0 and t == 0 and part is Ph),
                                                stop=(kp == 4 and t == 1 and part is Pl))
                        ins.then_inc(pv_done, 1)
                        if kp == 4:
                            pe.wait_ge(pv_done, j * STEPS + (m + 1))
                            pe.sem_inc(acc_done, 1)
                    if i in (1, 2, 4):
                        turn_k((1, 2, 4).index(i))
                    if i == 8:
                        gram()
                    if i in (12, 13, 15):
                        quadratic((12, 13, 15).index(i))
                    if i in (18, 19, 21):
                        total((18, 19, 21).index(i))

        steps_before = []

        def pairs_over(eng):
            eng.wait_ge(wqk_lo, PAIRS + 1)
            eng.wait_ge(pv_done, PAIRS * STEPS)
            eng.wait_ge(tmp_done, 6 * PAIRS)
            eng.wait_ge(o_fin, 3 * PAIRS)
            eng.wait_ge(o_store, 32 * PAIRS)

        @block.sync
        def _(sp):
            sp.dma_start(sbr[:], sb_.rearrange("(a d) -> a d", a=1).broadcast_to([T, E])).then_inc(bias_in, 16)
            sp.dma_start(swk[:], sw.rearrange("(k p) e -> p k e", p=P)).then_inc(bias_in, 16)
            pairs_over(sp)
            sp.dma_start(bgp[:], gnn_b.rearrange("(a d) -> a d", a=1).broadcast_to([T, D])).then_inc(bias_in, 16)

            def load_w3(wc):
                w, k = w_parts[wc // 3][0], 2 * (wc % 3)
                if wc >= 5:
                    sp.wait_ge(w_lo, wc - 1)
                sp.dma_start(wst3[:, wc % 2, :, :],
                             w[k * P:(k + 2) * P, :].rearrange("(k p) n -> p k n", p=P)).then_inc(w_in[wc % 2], 16)

            def load_counts(q):
                if 2 <= q < NT + 2:
                    sp.wait_ge(deg_mm, q - 1)
                if q >= NT + 2:
                    sp.wait_ge(csc_done, q - NT - 1)
                d = q % NT
                sp.dma_start(Cs[:, q % 2], counts[0:N * N].rearrange("(s p d) o -> p s (d o)", p=T, d=N)[
                    :, :, d * T:(d + 1) * T]).then_inc(cs_in[q % 2], 16)

            for wc in (3, 4, 5):
                load_w3(wc)
            sp.wait_ge(scattered, CLEARED + 16 * ET)
            for q in range(NT):
                load_counts(q)
            sp.wait_ge(h_mm, 2 * NT)
            for i in range(NT):
                sp.dma_start(xr[:, i % 2, :], x[i * T:(i + 1) * T, :]).then_inc(xr_in[i % 2], 16)
                if i == 0:
                    sp.dma_start(t0_[:, 1, :], b_proj.rearrange("(a d) -> a d", a=1).broadcast_to([T, D])
                                 ).then_inc(bias_in, 16)
                    load_w3(6)
                if i >= 1:
                    sp.wait_ge(pj_mm, i)
                sp.dma_start(oS[:].bitcast(F32).rearrange("p j l t -> p j (l t)"),
                             odram.rearrange("(j p) i l t -> p j i (l t)", p=P)[:, :, i, :]).then_inc(os_in, 16)
                if i == 0:
                    load_w3(7)
                    load_w3(8)
                load_counts(NT + i)
                if i >= 1:
                    sp.wait_ge(x1_done, i)
                    sp.dma_start(x1d[(i - 1) * T:i * T, :], t0_[:, (i - 1) % 2, :]).then_inc(x1_store[(i - 1) % 2], 16)
            sp.wait_ge(x1_done, NT)
            sp.dma_start(x1d[(NT - 1) * T:, :], t0_[:, (NT - 1) % 2, :]).then_inc(x1_store[(NT - 1) % 2], 16)

        @block.scalar
        def _(act):
            pairs_over(act)

            def split_w(wc):
                act.wait_ge(w_in[wc % 2], 16 * (wc // 2 + 1))
                if wc == 6:
                    act.wait_ge(h_mm, 2 * NT)
                act.activation(wH3[:, 2 * (wc % 3):2 * (wc % 3) + 2, :], wst3[:, wc % 2, :, :], ACT.Copy).then_inc(w_hi, 1)

            for wc in (3, 4, 5):
                split_w(wc)
            for g in range(2 * NT):
                i, c = g // 2, g % 2
                act.wait_ge(h_mm, g + 1)
                act.activation(HH[:, i, c * HALF:(c + 1) * HALF], ps[0:T, g % 4, 0:HALF], ACT.Copy).then_inc(h_hi, 1)
            for wc in (6, 7, 8):
                split_w(wc)
            act.wait_ge(var_ready, 2)
            act.activation(dtmp[:, 1, :], dtmp[:, 0, :], ACT.Sqrt).then_inc(dinv_sd, 1)

            def evac_xf(i):
                act.wait_ge(xf_tr, i + 1)
                if i >= 1:
                    act.wait_ge(lg_mm, i)
                act.activation(xfT[:, 0:4, :], ps[:, 6, 0:4 * T].rearrange("p (k t) -> p k t", t=T), ACT.Copy
                               ).then_inc(xf_evac, 1)
                act.activation(xfT[:, 4:6, :], ps[:, 7, 0:2 * T].rearrange("p (k t) -> p k t", t=T), ACT.Copy
                               ).then_inc(xf_evac, 1)

            def round_counts(i):
                act.wait_ge(csc_done, i + 1)
                if i >= 2:
                    act.wait_ge(agg_mm, i - 1)
                act.activation(CH[:, i % 2], Csc[:], ACT.Copy).then_inc(ch_done, 1)

            round_counts(0)
            for i in range(NT):
                if i + 1 < NT:
                    round_counts(i + 1)
                if i >= 1:
                    evac_xf(i - 1)
                act.wait_ge(var2, i + 1)
                act.activation(rs[:, 1, i:i + 1], rs[:, 0, i:i + 1], ACT.Sqrt).then_inc(sd2, 1)
            evac_xf(NT - 1)

        def newton(order, dve, r, sd, v, tmp):
            order(dve.reciprocal(r, sd))
            order(dve.tensor_tensor(tmp, r, r, ALU.mult))
            order(dve.tensor_tensor(tmp, tmp, v, ALU.mult))
            order(dve.tensor_scalar(tmp, tmp, -0.5, 1.5, ALU.mult, ALU.add))
            order(dve.tensor_tensor(r, r, tmp, ALU.mult))

        @block.vector
        def _(dve):
            pairs_over(dve)
            order = Chain(dve, route_order)

            def split_w(wc):
                dve.wait_ge(w_hi, wc + 1)
                k = 2 * (wc % 3)
                dve.tensor_tensor(wL3[:, k:k + 2, :], wst3[:, wc % 2, :, :], wH3[:, k:k + 2, :].bitcast(F32),
                                  ALU.subtract).then_inc(w_lo, 1)

            for wc in (3, 4, 5):
                split_w(wc)
            for g in range(2 * NT):
                i, c = g // 2, g % 2
                cs = slice(c * HALF, (c + 1) * HALF)
                dve.wait_ge(h_hi, g + 1)
                dve.tensor_tensor(HL[:, i, cs], ps[0:T, g % 4, 0:HALF], HH[:, i, cs].bitcast(F32),
                                  ALU.subtract).then_inc(h_lo, 1)
            for wc in (6, 7, 8):
                split_w(wc)
            dve.wait_ge(deg_mm, NT)
            dve.tensor_scalar(dtmp[:, 0, :], ps[0:T, 4, 0:2 * NT].rearrange("p (i a) -> p i a", a=2)[:, :, 0], 1.0, None,
                              ALU.add).then_inc(var_ready, 1)
            dve.wait_ge(dinv_sd, 1)
            newton(order, dve, dinv[:], dtmp[:, 1, :], dtmp[:, 0, :], dtmp[:, 2, :])

            def scale_counts(i):
                q = NT + i
                dve.wait_ge(cs_in[q % 2], 16 * (q // 2 + 1))
                order(dve.tensor_tensor(Cs[:, q % 2, i, :], Cs[:, q % 2, i, :], ident[0:T, 0:T], ALU.add))
                if i >= 1:
                    dve.wait_ge(cl_done, i)
                dve.tensor_tensor(Csc[:], Cs[:, q % 2], dinv[:].unsqueeze(2).broadcast_to([T, NT, T]),
                                  ALU.mult).then_inc(csc_done, 1)
                dve.wait_ge(ch_done, i + 1)
                if i >= 2:
                    dve.wait_ge(agg_mm, i - 1)
                dve.tensor_tensor(CL[:, i % 2], Csc[:], CH[:, i % 2].bitcast(F32), ALU.subtract).then_inc(cl_done, 1)

            def logits(i):
                dve.wait_ge(lg_mm, i + 1)
                dve.tensor_tensor(lg[:, 0, i, :], ps[0:T, 7, 384:384 + E], sbr[:], ALU.add).then_inc(lg_done, 1)

            scale_counts(0)
            dve.wait_ge(bias_in, 64)
            order(dve.tensor_tensor(bgp[:], bgp[:], t0_[:, 1, :], ALU.add))
            for i in range(NT):
                t_ = t0_[:, i % 2, :]
                th = t_.rearrange("p (c n) -> p c n", c=2)
                if i >= 2:
                    dve.wait_ge(x1_store[i % 2], 16 * (i // 2))
                dve.wait_ge(xr_in[i % 2], 16 * (i // 2 + 1))
                order(dve.tensor_tensor(t_, xr[:, i % 2, :], bgp[:], ALU.add))
                dve.wait_ge(pj_mm, i + 1)
                dve.tensor_tensor(th, ps[0:T, 4:6, 0:HALF], th, ALU.add).then_inc(pj_read, 1)
                if i + 1 < NT:
                    scale_counts(i + 1)
                dve.wait_ge(pj_read, i + 1)
                dve.wait_ge(agg_mm, i + 1)
                b = 2 * (i % 2)
                dve.scalar_tensor_tensor(out=th, in0=ps[0:T, b:b + 2, 0:HALF], scalar=dinv[:, i:i + 1], in1=th,
                                         op0=ALU.mult, op1=ALU.add).then_inc(x1_done, 1)
                dve.wait_ge(x1_done, i + 1)
                for c in range(2):
                    dve.bn_stats(stats[:, i, c, :], t_[:, c * HALF:(c + 1) * HALF]).then_inc(st_done, 1)
                dve.wait_ge(st_done, 2 * NT + 2 * i + 2)
                order(dve.bn_aggr(mv[:, i, :], stats[:, i]))
                dve.tensor_scalar(rs[:, 0, i:i + 1], mv[:, i, 1:2], EPS, None, ALU.add).then_inc(var2, 1)
                if i >= 1:
                    logits(i - 1)
                dve.wait_ge(sd2, i + 1)
                newton(order, dve, rs[:, 2, i:i + 1], rs[:, 1, i:i + 1], rs[:, 0, i:i + 1], rs[:, 3, i:i + 1])
                dve.tensor_scalar(XF[:, i, :], t_, mv[:, i, 0:1], rs[:, 2, i:i + 1], ALU.subtract,
                                  ALU.mult).then_inc(xf_done, 1)
            logits(NT - 1)
            steps_before.append(order.n)

        @block.tensor
        def _(pe):
            pairs_over(pe)
            pe.wait_ge(oacc_done, 6 * PAIRS + FREE)
            pe.wait_ge(w_lo, 6)
            for g in range(2 * NT):
                i, c = g // 2, g % 2
                if g >= 4:
                    pe.wait_ge(h_lo, g - 3)
                product(pe, ps[0:T, g % 4, 0:HALF],
                        lambda k: (XH[:, k, i * T:(i + 1) * T], XL[:, k, i * T:(i + 1) * T]),
                        lambda k: (wH3[:, k, c * HALF:(c + 1) * HALF], wL3[:, k, c * HALF:(c + 1) * HALF]),
                        KT).then_inc(h_mm, 1)
                if c == 1:
                    pe.wait_ge(cs_in[i % 2], 16 * (i // 2 + 1))
                    for s in range(NT):
                        ins = pe.matmul(ps[0:T, 4, 2 * i:2 * i + 2], Cs[:, i % 2, s, :], ones2[:], start=(s == 0),
                                        stop=(s == NT - 1))
                    ins.then_inc(deg_mm, 1)

            def transposes(i):
                pe.wait_ge(xf_done, i + 1)
                if i >= 1:
                    pe.wait_ge(lg_done, i)
                for k in range(KT):
                    ins = pe.transpose(ps[:, 6 + k // 4, (k % 4) * T:(k % 4 + 1) * T], XF[:, i, k * P:(k + 1) * P],
                                       ident[0:T, 0:T])
                ins.then_inc(xf_tr, 1)

            def logits(i):
                pe.wait_ge(xf_evac, 2 * i + 2)
                for k in range(KT):
                    ins = pe.matmul(ps[0:T, 7, 384:384 + E], xfT[:, k, :], swk[:, k, :], start=(k == 0),
                                    stop=(k == KT - 1))
                ins.then_inc(lg_mm, 1)

            pe.wait_ge(dinv_sd, 1)
            pe.wait_ge(h_lo, 2 * NT)
            pe.wait_ge(w_lo, 9)
            for i in range(NT):
                pe.wait_ge(os_in, 16 * i + 16)
                if i >= 1:
                    pe.wait_ge(pj_read, i)
                for c in range(2):
                    ins = product(pe, ps[0:T, 4 + c, 0:HALF], lambda k: (oS[:, k, 0, :], oS[:, k, 1, :]),
                                  lambda k: (wH3[:, k, c * HALF:(c + 1) * HALF], wL3[:, k, c * HALF:(c + 1) * HALF]), KT)
                ins.then_inc(pj_mm, 1)
                if i >= 1:
                    transposes(i - 1)
                pe.wait_ge(cl_done, i + 1)
                if i >= 2:
                    pe.wait_ge(x1_done, i - 1)
                for c in range(2):
                    ins = product(pe, ps[0:T, 2 * (i % 2) + c, 0:HALF],
                                  lambda s: (CH[:, i % 2, s, :], CL[:, i % 2, s, :]),
                                  lambda s: (HH[:, s, c * HALF:(c + 1) * HALF], HL[:, s, c * HALF:(c + 1) * HALF]), NT)
                ins.then_inc(agg_mm, 1)
                if i >= 1:
                    logits(i - 1)
            transposes(NT - 1)
            logits(NT - 1)

        def nodes_over(eng):
            eng.wait_ge(agg_mm, NT)
            eng.wait_ge(pj_mm, NT)
            eng.wait_ge(lg_mm, NT)
            eng.wait_ge(cl_done, NT)
            eng.wait_ge(xf_done, NT)
            eng.wait_ge(lg_done, NT)
            eng.wait_ge(x1_store[0], 80)
            eng.wait_ge(x1_store[1], 80)

        LASTM = E // 2 - 1

        @block.sync
        def _(sp):
            def load_expert(e, n):
                if n is not None:
                    sp.wait_ge(we_lo, n)
                sp.dma_start(w1s[:], w1.rearrange("e d f -> (e d) f")[at(e * D, D)].rearrange("(k p) f -> p k f", p=P)).then_inc(we_in, 16)
                sp.dma_start(w2s[:], w2.rearrange("e d f -> (e d) f")[at(e * F, F)].rearrange("(k p) f -> p k f", p=P)).then_inc(we_in, 16)

            def load_rows(e, b):
                for t, (r0, n) in enumerate(CTILES):
                    sp.dma_start(xe[0:n, b, t, :], rows[at(e * CAP + r0, n), :]).then_inc(xe_in[b], 16)
                sp.dma_start(b2r[:, b, :], b2[at(e, 1), :].broadcast_to([98, D])).then_inc(b2_in[b], 16)

            def store_rows(e):
                for t, (r0, n) in enumerate(CTILES):
                    sp.wait_ge(oe_done, 2 * e + (t + 1 + FREE))
                    sp.dma_start(rows[at(e * CAP + r0, n), :], oE[0:n, t, :]).then_inc(oe_store, 16)
                sp.wait_ge(oe_store, 32 * e + 32)
                sp.sem_inc(oe_free, 2)

            nodes_over(sp)
            sp.sem_inc(oe_free, 2)
            sp.dma_start(b1row[:], b1.rearrange("e (m p) -> (e m) p", p=P)).then_inc(b1_in, 16)
            load_expert(0, None)
            load_expert(1, 1)
            sp.wait_ge(sent, 16 * NT)
            load_rows(0, 0)

            def turn(m, last):
                for b in range(2):
                    e = 2 * m + b
                    if not (last and b == 1):
                        sp.wait_ge(xe_tr, 3 * e + 3)
                        load_rows(e + 1, 1 - b)
                    if not last:
                        load_expert(e + 2, 2 * m + (b + 2))
                    store_rows(e)

            with sp.Fori(0, LASTM) as m:
                turn(m, False)
            turn(LASTM, True)

        @block.gpsimd
        def _(pool):
            pool.wait_ge(slot_done, 1)
            pool.wait_ge(xf_done, NT)
            pool.wait_ge(r_zero, 32)
            for i in range(NT):
                if i >= 1:
                    pool.wait_ge(sent, 16 * i)
                pool.indirect_dma_start(out=rows, out_offset=bass.IndirectOffsetOnAxis(ap=slots[:, i:i + 1], axis=0),
                                        in_=XF[:, i, :], in_offset=None).then_inc(sent, 16)

        @block.scalar
        def _(act):
            nodes_over(act)

            def split_expert(n, b):
                act.wait_ge(we_in, n * 32)
                act.activation(w1H[:, b], w1s[:], ACT.Copy).then_inc(we_hi, 1)
                act.activation(w2H[:, b], w2s[:], ACT.Copy).then_inc(we_hi, 1)

            split_expert(1, 0)
            act.wait_ge(dm_done, 1)
            act.activation(lg[:, 2], lg[:, 1], ACT.Exp).then_inc(ex_done, 1)
            for n, (t0, nt) in enumerate(GROUPS):
                act.wait_ge(pm_mm, n + 1)
                act.activation(PM[:, t0 * T:(t0 + nt) * T], ps[0:T, n, 0:nt * T], ACT.Copy).then_inc(pm_evac, 1)

            def cut_rows(e):
                for n in range(3):
                    act.wait_ge(xe_tr, 3 * e + (n + 1))
                    act.activation(xeH[:, 2 * n:2 * n + 2, 0:CAP],
                                   ps[:, n, 0:2 * CAPP].rearrange("p (k c) -> p k c", k=2)[:, :, 0:CAP],
                                   ACT.Copy).then_inc(xe_hi, 1)

            act.wait_ge(pads, 1)
            cut_rows(0)

            def turn(m, last):
                for b in range(2):
                    e = 2 * m + b
                    act.wait_ge(b1cur_done, e + 1)
                    for f in range(FT):
                        act.wait_ge(m1_mm, 3 * e + (f + 1))
                        act.activation(h32[:, f, :], ps[:, 3 + f, 0:CAPP], ACT.Gelu,
                                       bias=b1cur[:, b, f:f + 1]).then_inc(h_act, 1)
                        act.wait_ge(h_act, 3 * e + (f + 1))
                        act.activation(hH[:, f, :], h32[:, f, :], ACT.Copy).then_inc(hh_done, 1)
                    if not (last and b == 1):
                        cut_rows(e + 1)
                        split_expert(2 * m + (b + 2), 1 - b)

            with act.Fori(0, LASTM) as m:
                turn(m, False)
            turn(LASTM, True)

        @block.vector
        def _(dve):
            nodes_over(dve)
            order = Chain(dve, route_order, steps_before[0])

            def split_expert(n, b):
                dve.wait_ge(we_hi, n * 2)
                dve.tensor_tensor(w1L[:, b], w1s[:], w1H[:, b].bitcast(F32), ALU.subtract).then_inc(we_lo1, 1)
                dve.tensor_tensor(w2L[:, b], w2s[:], w2H[:, b].bitcast(F32), ALU.subtract).then_inc(we_lo, 1)

            def wide(a):
                return a.unsqueeze(2).broadcast_to([T, NT, E])

            top, pm, route, rank, kept, slot, slotf, tok, sm = (rt[:, n, :] for n in range(9))
            eid = iota_f[:, 16:16 + E].unsqueeze(1).broadcast_to([T, NT, E])
            order(dve.tensor_reduce(top, lg[:, 0], AX.X, ALU.max))
            dve.tensor_tensor(lg[:, 1], lg[:, 0], wide(top), ALU.subtract).then_inc(dm_done, 1)
            dve.wait_ge(dm_done, 1)
            order(dve.tensor_scalar(lg[:, 3], lg[:, 1], 0.0, None, ALU.is_ge))
            order(dve.scalar_tensor_tensor(out=lg[:, 4], in0=lg[:, 3], scalar=-100.0, in1=eid, op0=ALU.mult, op1=ALU.add))
            order(dve.tensor_reduce(route, lg[:, 4], AX.X, ALU.min))
            order(dve.tensor_scalar(route, route, 100.0, None, ALU.add))
            order(dve.tensor_tensor(lg[:, 3], eid, wide(route), ALU.is_equal))
            order(dve.tensor_copy(ohb[:], lg[:, 3]))
            dve.wait_ge(ex_done, 1)
            order(dve.tensor_reduce(sm, lg[:, 2], AX.X, ALU.add))
            dve.reciprocal(pm, sm).then_inc(pm_done, 1)
            split_expert(1, 0)
            dve.memset(xeH[:, :, CAP:].bitcast(F32), 0.0)
            dve.memset(xeL[:, :, CAP:].bitcast(F32), 0.0).then_inc(pads, 1)
            dve.wait_ge(pm_evac, len(GROUPS))
            for jt in range(NT):
                mine = pm[:, jt:jt + 1]
                lo, hi = jt * T, (jt + 1) * T
                dve.scalar_tensor_tensor(out=same[:, jt % 2, :], in0=PM[:, lo:hi], scalar=mine, in1=later[:],
                                         op0=ALU.is_equal, op1=ALU.mult).then_inc(same_done, 1)
                if jt > 0:
                    dve.tensor_scalar(Bt[:, jt, 0:lo], PM[:, 0:lo], mine, None, ALU.is_lt).then_inc(b_done, 1)
                if jt < NT - 1:
                    dve.tensor_scalar(Bt[:, jt, hi:], PM[:, hi:], mine, None, ALU.is_le).then_inc(b_done, 1)
                dve.wait_ge(same_done, jt + 1)
                dve.scalar_tensor_tensor(out=Bt[:, jt, lo:hi], in0=PM[:, lo:hi], scalar=mine, in1=same[:, jt % 2, :],
                                         op0=ALU.is_lt, op1=ALU.add).then_inc(b_done, 1)
            dve.wait_ge(cnt_mm, 1)
            order(dve.tensor_tensor(lg[:, 4], ps[0:T, 3, 0:NT * E].rearrange("p (i e) -> p i e", e=E), lg[:, 3], ALU.mult))
            order(dve.tensor_reduce(rank, lg[:, 4], AX.X, ALU.add))
            order(dve.tensor_scalar(kept, rank, float(CAP), None, ALU.is_lt))
            order(dve.scalar_tensor_tensor(out=slot, in0=route, scalar=float(CAP), in1=rank, op0=ALU.mult, op1=ALU.add))
            order(dve.tensor_scalar(tok, iota_f[:, 0:NT], float(SLOTS), None, ALU.add))
            order(dve.tensor_tensor(slot, slot, tok, ALU.subtract))
            order(dve.tensor_tensor(slot, slot, kept, ALU.mult))
            order(dve.tensor_tensor(slotf, slot, tok, ALU.add))
            dve.tensor_copy(slots[:], slotf).then_inc(slot_done, 1)
            dve.wait_ge(b1_tr, 1)
            dve.tensor_copy(b1c[:].rearrange("p e m -> p (e m)"), ps[:, 3, 256:256 + E * FT]).then_inc(b1_done, 1)
            dve.wait_ge(b1_done, 1)

            def bias_of(e, b):
                dve.tensor_scalar(b1cur[:, b, :], b1c[:, at(e, 1), :].rearrange("p o m -> p (o m)"), 1.0, None,
                                  ALU.mult).then_inc(b1cur_done, 1)

            def cut_rows(e):
                for n in range(3):
                    dve.wait_ge(xe_hi, 3 * e + (n + 1))
                    dve.tensor_tensor(xeL[:, 2 * n:2 * n + 2, 0:CAP],
                                      ps[:, n, 0:2 * CAPP].rearrange("p (k c) -> p k c", k=2)[:, :, 0:CAP],
                                      xeH[:, 2 * n:2 * n + 2, 0:CAP].bitcast(F32), ALU.subtract).then_inc(xe_lo, 1)

            dve.sem_inc(oe_done, FREE)
            bias_of(0, 0)
            cut_rows(0)

            def turn(m, last):
                for b in range(2):
                    e = 2 * m + b
                    for f in range(FT):
                        dve.wait_ge(hh_done, 3 * e + (f + 1))
                        dve.tensor_tensor(hL[:, f, :], h32[:, f, :], hH[:, f, :].bitcast(F32),
                                          ALU.subtract).then_inc(hl_done, 1)
                    if not (last and b == 1):
                        bias_of(e + 1, 1 - b)
                        cut_rows(e + 1)
                        split_expert(2 * m + (b + 2), 1 - b)
                    dve.wait_ge(b2_in[b], m * 16 + 16)
                    for t, (r0, n) in enumerate(CTILES):
                        dve.wait_ge(m2_mm, 2 * e + (t + 1))
                        dve.wait_ge(oe_free, 2 * e + (t + FREE))
                        dve.tensor_tensor(oE[0:n, t, :].rearrange("p (c d) -> p c d", c=2),
                                          ps[0:n, 6 - 2 * t:8 - 2 * t, 0:HALF],
                                          b2r[0:n, b, :].rearrange("p (c d) -> p c d", c=2), ALU.add).then_inc(oe_done, 1)

            with dve.Fori(0, LASTM) as m:
                turn(m, False)
            turn(LASTM, True)

        @block.tensor
        def _(pe):
            nodes_over(pe)
            pe.wait_ge(b1_in, 16)
            pe.transpose(ps[:, 3, 256:256 + E * FT], b1row[:], ident[0:E * FT, 0:E * FT]).then_inc(b1_tr, 1)
            pe.wait_ge(pm_done, 1)
            for n, (t0, nt) in enumerate(GROUPS):
                for t in range(nt):
                    i = t0 + t
                    ins = pe.matmul(ps[0:T, n, t * T:(t + 1) * T], rt[:, 1, i:i + 1].broadcast_to([T, T]),
                                    ident[0:T, 0:T], start=True, stop=True)
                ins.then_inc(pm_mm, 1)
            pe.wait_ge(b_done, 3 * NT - 2)
            for i in range(NT):
                for jt in range(NT):
                    ins = pe.matmul(ps[0:T, 3, i * E:(i + 1) * E], Bt[:, jt, i * T:(i + 1) * T], ohb[:, jt, :],
                                    start=(jt == 0), stop=(jt == NT - 1))
            ins.then_inc(cnt_mm, 1)

            def turn_rows(e, b, n_in):
                pe.wait_ge(xe_in[b], n_in)
                for n in range(3):
                    for k in range(2):
                        for t, (r0, cnt) in enumerate(CTILES):
                            f = 2 * n + k
                            ins = pe.transpose(ps[:, n, k * CAPP + r0:k * CAPP + r0 + cnt],
                                               xe[0:cnt, b, t, f * P:(f + 1) * P], ident[0:cnt, 0:cnt])
                    ins.then_inc(xe_tr, 1)

            turn_rows(0, 0, 32)

            def turn(m, last):
                for b in range(2):
                    e = 2 * m + b
                    pe.wait_ge(xe_lo, 3 * e + 3)
                    pe.wait_ge(we_lo, e + 1)
                    for f in range(FT):
                        if f == 0:
                            pe.wait_ge(b1_done, 1)
                        elif f == 1:
                            pe.wait_ge(oe_done, 2 * e + FREE)
                        product(pe, ps[:, 3 + f, 0:CAPP],
                                lambda k: (w1H[:, b, k, f * P:(f + 1) * P], w1L[:, b, k, f * P:(f + 1) * P]),
                                lambda k: (xeH[:, k, :], xeL[:, k, :]), KT).then_inc(m1_mm, 1)
                    if not (last and b == 1):
                        turn_rows(e + 1, 1 - b, m * 32 + 32 * (b + 1))
                    pe.wait_ge(hl_done, 3 * e + 3)
                    for t, (r0, n) in enumerate(CTILES):
                        for c in range(2):
                            ins = product(pe, ps[0:n, 6 - 2 * t + c, 0:HALF],
                                          lambda f: (hH[:, f, r0:r0 + n], hL[:, f, r0:r0 + n]),
                                          lambda f: (w2H[:, b, f, c * HALF:(c + 1) * HALF],
                                                     w2L[:, b, f, c * HALF:(c + 1) * HALF]), FT)
                        ins.then_inc(m2_mm, 1)

            with pe.Fori(0, LASTM) as m:
                turn(m, False)
            turn(LASTM, True)

        @block.sync
        def _(sp):
            sp.wait_ge(sent, 16 * NT)
            sp.dma_start(XF[:], x1d.rearrange("(i p) d -> p i d", p=T)).then_inc(x1_back, 16)
            for i in range(NT):
                sp.wait_ge(out_done, i + 1)
                sp.dma_start(out[i * T:(i + 1) * T, :], yg[:, i, :]).then_inc(stored, 16)
            sp.wait_ge(stored, 16 * NT)
            sp.wait_ge(oe_store, 32 * E)

        @block.gpsimd
        def _(pool):
            pool.wait_ge(oe_store, 32 * E)
            pool.wait_ge(we_lo, E)
            pool.wait_ge(m2_mm, 2 * E)
            for i in range(NT):
                pool.indirect_dma_start(out=yg[:, i, :], out_offset=None, in_=rows,
                                        in_offset=bass.IndirectOffsetOnAxis(ap=slots[:, i:i + 1], axis=0)
                                        ).then_inc(got[i], 16)

        @block.vector
        def _(dve):
            dve.wait_ge(x1_back, 16)
            for i in range(NT):
                dve.wait_ge(got[i], 16)
                dve.scalar_tensor_tensor(out=yg[:, i, :], in0=yg[:, i, :], scalar=rt[:, 1, i:i + 1], in1=XF[:, i, :],
                                         op0=ALU.mult, op1=ALU.add).then_inc(out_done, 1)


def product(pe, out, left, right, tiles):
    for k in range(tiles):
        lh, ll = left(k)
        rh, rl = right(k)
        pe.matmul(out, lh, rh, start=(k == 0), stop=False)
        pe.matmul(out, lh, rl, start=False, stop=False)
        ins = pe.matmul(out, ll, rh, start=False, stop=(k == tiles - 1))
    return ins


_INS = ["x", "src", "dst", "L0_gnn_W", "L0_gnn_b", "L0_mix_w_qkv", "L0_mix_b_qkv", "L0_mix_w_proj",
        "L0_mix_b_proj", "L0_ffn_switch_w", "L0_ffn_switch_b", "L0_ffn_w1", "L0_ffn_b1", "L0_ffn_w2",
        "L0_ffn_b2"]


def kernel(**inputs):
    import numpy as _np
    import concourse.bacc as _bacc
    from concourse.bass_utils import run_bass_kernel_spmd as _run

    nc = _bacc.Bacc("TRN2", target_bir_lowering=False, num_devices=1)
    arrays, args = {}, []
    for name in _INS:
        a = _np.ascontiguousarray(inputs[name])
        arrays[name] = a
        args.append(nc.dram_tensor(name, a.shape, mybir.dt.from_np(a.dtype), kind="ExternalInput").ap())
    result = nc.dram_tensor("out", (N, D), F32, kind="ExternalOutput").ap()
    counts = nc.dram_tensor("counts", (N * N + T, 1), F32, kind="Internal").ap()
    keyd = nc.dram_tensor("keyd", (EROWS, 250), F32, kind="Internal").ap()
    vdram = nc.dram_tensor("vdram", (PAIRS * T, NT, 4 * HD), F32, kind="Internal").ap()
    odram = nc.dram_tensor("odram", (PAIRS * P, NT, 2, T), F32, kind="Internal").ap()
    rows = nc.dram_tensor("rows", (SLOTS + N, D), F32, kind="Internal").ap()
    x1d = nc.dram_tensor("x1d", (N, D), F32, kind="Internal").ap()
    build(nc, *args, result, counts, keyd, vdram, odram, rows, x1d)
    return _run(nc, [arrays], core_ids=[0]).results[0]["out"]
```

```python
from contextlib import ExitStack

import concourse.bass as bass
from concourse import mybir

F32 = mybir.dt.float32
F32R = mybir.dt.float32r
BF16 = mybir.dt.bfloat16
I32 = mybir.dt.int32
U32 = mybir.dt.uint32
ALU = mybir.AluOpType
ACT = mybir.ActivationFunctionType
AX = mybir.AxisListType

P = 128
N, D = 1250, 768
T, NT = 125, 10
KT = D // P
HALF = D // 2
H, HD = 12, 64
PAIRS = H // 2
SCALE = HD ** -0.5
EPS = 1e-5
CHUNKS = [(0, 418), (418, 416), (834, 416)]
CW = 418
EDGES = 20000
ET = EDGES // T
EC, EU = 16, ET // 16
EROWS = 80
CLEARED = 32
AGAIN = 256.0
E, F = 8, 384
FT = F // P
CAP = int(1.25 * N / E)
SLOTS = E * CAP
CAPP = CAP + 1
CTILES = [(0, 98), (98, 97)]
STEPS = 30
LAG = 3
RING = 3


class Chain:

    def __init__(self, eng, sem, base=0):
        self.eng, self.sem, self.base, self.n = eng, sem, base, 0

    def __call__(self, ins):
        self.n += 1
        ins.then_inc(self.sem, 1)
        self.eng.wait_ge(self.sem, self.base + self.n)


def at(start, size):
    return bass.ds(start, size)


def build(nc, x, src, dst, gnn_w, gnn_b, w_qkv, b_qkv, w_proj, b_proj, sw, sb_, w1, b1, w2, b2, out,
          counts, keyd, vdram, odram, rows, x1d):
    ctx = ExitStack()
    with ctx:
        def sem(name):
            return ctx.enter_context(nc.semaphore(name))

        def keep(name, shape, dt):
            return ctx.enter_context(nc.sbuf_tensor(name, shape, dt))

        def region(specs):
            with ExitStack() as inner:
                return [inner.enter_context(nc.sbuf_tensor(*s)) for s in specs]

        def left(stack, specs):
            return [stack.enter_context(nc.sbuf_tensor(*s)) for s in specs]

        def right(stack, specs):
            return [stack.enter_context(nc.sbuf_tensor(*s, side="right")) for s in specs]

        ps = ctx.enter_context(nc.psum_tensor("ps", [P, 8, 512], F32))

        ident = keep("ident", [P, P], F32)
        blocks = keep("blocks", [P, P], F32)
        ones2 = keep("ones2", [T, 2], F32)
        later = keep("later", [T, T], F32)
        iota_i = keep("iota_i", [T, 32], I32)
        iota_f = keep("iota_f", [T, 32], F32)
        countc = keep("countc", [T, ET], F32)
        idxf = keep("idxf", [T, ET], F32)
        icur = keep("icur", [T, 2], U32)
        vcur = keep("vcur", [T, 2], F32)
        stats = keep("stats", [T, NT, 2, 6], F32)
        mv = keep("mv", [T, NT, 2], F32)
        rs = keep("rs", [T, 4, NT], F32)
        bcols = keep("bcols", [P, 3, PAIRS + 1], F32)
        pbias = keep("pbias", [P, 2], F32)
        dinv = keep("dinv", [T, NT], F32)
        dtmp = keep("dtmp", [T, 4, NT], F32)
        swk, sbr = keep("swk", [P, KT, E], F32), keep("sbr", [T, E], F32)
        lg = keep("lg", [T, 6, NT, E], F32)
        rt = keep("rt", [T, 10, NT], F32)
        ohb = keep("ohb", [T, NT, E], BF16)
        slots = keep("slots", [T, NT], U32)
        b1c, b1cur = keep("b1c", [P, E, FT], F32), keep("b1cur", [P, 2, FT], F32)

        x_in = [sem(f"x_in{i}") for i in range(NT)]
        e_in, b_in = sem("e_in"), sem("b_in")
        key_out, kb_in = sem("key_out"), [sem("kb_in0"), sem("kb_in1")]
        r_zero = sem("r_zero")
        w_in = [sem("w_in0"), sem("w_in1")]
        v_store = [sem("v_store0"), sem("v_store1")]
        o_store = sem("o_store")
        scattered = sem("scattered")
        consts, carrier = sem("consts"), sem("carrier")
        pool_order, dve_order = sem("pool_order"), sem("dve_order")
        keys, key_tr, keyc_done, idx_ready = sem("keys"), sem("key_tr"), sem("keyc_done"), sem("idx_ready")
        eq_done = sem("eq_done")
        st_done, var_ready, sd_ready, xn_done = sem("st_done"), sem("var_ready"), sem("sd_ready"), sem("xn_done")
        tr_done, xt_hi, xt_lo = sem("tr_done"), sem("xt_hi"), sem("xt_lo")
        w_hi, w_lo = sem("w_hi"), sem("w_lo")
        v_mm, v_hi, v_lo = sem("v_mm"), sem("v_hi"), sem("v_lo")

        features, pair_weights, hidden_weights, node_work = ExitStack(), ExitStack(), ExitStack(), ExitStack()
        XH, XL = right(features, [("XH", [P, KT, N], F32R), ("XL", [P, KT, N], F32R)])
        ws, wqkH, wqkL = right(pair_weights, [("ws", [P, 2, KT, P], F32), ("wqkH", [P, 2, KT, P], F32R),
                                              ("wqkL", [P, 2, KT, P], F32R)])
        (xn, zeros, ekeys, key_t, kb, wst, wH, wL, VS, brow, triw, keyc, etmp) = region([
            ("xn", [T, NT, D], F32), ("zeros", [T, N], F32),
            ("ekeys", [EROWS, 2, 250], I32), ("key_t", [EROWS, 250], F32),
            ("kb", [T, 2, EC, T], F32), ("wst", [P, 2, 2, D], F32),
            ("wH", [P, KT, D], F32R), ("wL", [P, KT, D], F32R),
            ("VS", [T, 2, H, 2, HD], F32R), ("brow", [3 * PAIRS, P], F32),
            ("triw", [T, T], F32),
            ("keyc", [T, ET], F32), ("etmp", [T, 3, EC], F32)])

        (K32, kt2, KHA, KLA, MA, gs, Q32, OUN, R32, rden, vsb, tmpo, Pf, Ph, Pl, k1, inv, KHB, KLB, MB, OHL) = region([
            ("K32", [P, N], F32), ("kt2", [T, NT, 2, P], F32R),
            ("KHA", [P, N], F32R), ("KLA", [P, N], F32R), ("MA", [P, N], F32R), ("gs", [P, 3, P], F32),
            ("Q32", [P, N], F32), ("OUN", [P, N], F32), ("R32", [P, NT * P], F32), ("rden", [P, N], F32),
            ("vsb", [T, NT, 2, P], F32R), ("tmpo", [HD, 2, CW], F32),
            ("Pf", [T, RING, 2, CW], F32), ("Ph", [T, RING, 2, CW], F32R), ("Pl", [T, RING, 2, CW], F32R),
            ("k1", [P, 4], F32), ("inv", [T, NT, 2], F32),
            ("KHB", [P, N], F32R), ("KLB", [P, N], F32R), ("MB", [P, N], F32R),
            ("OHL", [P, 2, N], F32R)])
        KH, KL, MQ = (KHA, KHB), (KLA, KLB), (MA, MB)
        wqk_in, v_in = [sem("wqk_in0"), sem("wqk_in1")], [sem("v_in0"), sem("v_in1")]
        wqk_hi, wqk_lo, bias_ready = sem("wqk_hi"), sem("wqk_lo"), sem("bias_ready")
        qk_mm, kq_full, k_twice = sem("qk_mm"), sem("kq_full"), sem("k_twice")
        k_hi, k_lo, q_hi, q_lo = ([sem(f"{n}{a}") for a in range(2)] for n in ("k_hi", "k_lo", "q_hi", "q_lo"))
        sc_done, sq_done, p_hiA, p_hiD, p_lo, pv_done = (
            sem("sc_done"), sem("sq_done"), sem("p_hiA"), sem("p_hiD"), sem("p_lo"), sem("pv_done"))
        tmp_done, oacc_done = sem("tmp_done"), sem("oacc_done")
        kt_mm, kt_hi, kt_lo, g_mm, gfin_done = sem("kt_mm"), sem("kt_hi"), sem("kt_lo"), sem("g_mm"), sem("gfin_done")
        gq_mm, r_done, den_mm, inv_done, inv_wide, inv_mm, rden_done = (
            sem("gq_mm"), sem("r_done"), sem("den_mm"), sem("inv_done"), sem("inv_wide"), sem("inv_mm"),
            sem("rden_done"))
        o_fin, ohl_free, pair_order = sem("o_fin"), sem("ohl_free"), sem("pair_order")

        pair_weights.close()
        third = ExitStack()
        wst3, wL3, bgp, HH, HL, Cs, wpH, csum = left(third, [
            ("wst3", [P, 2, 2, D], F32), ("wL3", [P, KT, D], F32R), ("bgp", [T, D], F32),
            ("HH", [T, NT, D], F32R), ("HL", [T, NT, D], F32R), ("Cs", [T, 2, NT, T], F32),
            ("wpH", [P, KT, D], F32R), ("csum", [T, 2, T], F32)])
        wH3, = right(hidden_weights, [("wH3", [P, KT, D], F32R)])
        hidden_weights.close()
        features.close()
        XF, = right(ctx, [("XF", [T, NT, D], F32)])
        Csc, CH, CL, oS, xr, t0_, xfT = right(node_work, [
            ("Csc", [T, NT, T], F32), ("CH", [T, 2, NT, T], F32R), ("CL", [T, 2, NT, T], F32R),
            ("oS", [P, PAIRS, 2, T], F32R), ("xr", [T, 2, D], F32), ("t0_", [T, 2, D], F32),
            ("xfT", [P, KT, T], F32)])
        third.close()
        node_work.close()
        h_mm, h_hi, h_lo, deg_mm, dinv_sd, csum_done = (sem("h_mm"), sem("h_hi"), sem("h_lo"), sem("deg_mm"),
                                                        sem("dinv_sd"), sem("csum_done"))
        cs_in, xr_in = [sem("cs_in0"), sem("cs_in1")], [sem("xr_in0"), sem("xr_in1")]
        os_in, bias_in, x1_store = sem("os_in"), sem("bias_in"), [sem("x1_store0"), sem("x1_store1")]
        csc_done, ch_done, cl_done = sem("csc_done"), sem("ch_done"), sem("cl_done")
        pj_mm, agg_read, agg_mm, x1_done = sem("pj_mm"), sem("agg_read"), sem("agg_mm"), sem("x1_done")
        var2, sd2, xf_done, xf_tr, xf_evac, lg_mm, lg_done = (sem("var2"), sem("sd2"), sem("xf_done"), sem("xf_tr"),
                                                              sem("xf_evac"), sem("lg_mm"), sem("lg_done"))
        (w1s, w2s, w1H, w1L, w2H, w2L, xe, xeH, xeL, h32, hH, hL, oE, b2r, Bt, PM, b1row, same) = region([
            ("w1s", [P, KT, F], F32), ("w2s", [P, FT, D], F32),
            ("w1H", [P, 2, KT, F], F32R), ("w1L", [P, 2, KT, F], F32R),
            ("w2H", [P, 2, FT, D], F32R), ("w2L", [P, 2, FT, D], F32R),
            ("xe", [98, 2, 2, D], F32), ("xeH", [P, KT, CAPP], F32R), ("xeL", [P, KT, CAPP], F32R),
            ("h32", [P, FT, CAPP], F32), ("hH", [P, FT, CAPP], F32R), ("hL", [P, FT, CAPP], F32R),
            ("oE", [98, 2, D], F32), ("b2r", [98, 2, D], F32), ("Bt", [T, NT, N], BF16), ("PM", [T, N], F32),
            ("b1row", [E * FT, P], F32), ("same", [T, 2, T], F32)])
        ex_done, pm_done, pm_mm, pm_evac, b_done, cnt_mm, slot_done = (
            sem("ex_done"), sem("pm_done"), sem("pm_mm"), sem("pm_evac"), sem("b_done"), sem("cnt_mm"), sem("slot_done"))
        dm_done, route_order = sem("dm_done"), sem("route_order")
        sent = sem("sent")
        b1_in, b1_tr, b1_done, b1cur_done = sem("b1_in"), sem("b1_tr"), sem("b1_done"), sem("b1cur_done")
        we_hi, we_lo = sem("we_hi"), sem("we_lo")
        xe_in, b2_in = [sem("xe_in0"), sem("xe_in1")], [sem("b2_in0"), sem("b2_in1")]
        xe_tr, xe_hi, xe_lo, m1_mm, h_act, hh_done, hl_done, m2_mm, oe_done, oe_store = (
            sem("xe_tr"), sem("xe_hi"), sem("xe_lo"), sem("m1_mm"), sem("h_act"), sem("hh_done"), sem("hl_done"),
            sem("m2_mm"), sem("oe_done"), sem("oe_store"))
        pads, same_done = sem("pads"), sem("same_done")
        yg, = region([("yg", [T, NT, D], F32)])
        GOT = [0, 0, 1, 1, 2, 2, 3, 3, 4, 5]
        got = [sem(f"got{i}") for i in range(6)]
        x1_back, out_done, stored = sem("x1_back"), sem("out_done"), sem("stored")

        block = ctx.enter_context(nc.Block())

        w_parts = [(w_qkv[:, 2 * D:3 * D], 0), (gnn_w, 1), (w_proj, 2)]
        GROUPS = [(0, 4), (4, 4), (8, 2)]

        @block.sync
        def _(sp):
            for i in range(NT):
                sp.dma_start(xn[:, i, :], x[i * T:(i + 1) * T, :]).then_inc(x_in[i], 16)
                if i == 1:
                    sp.dma_start(ekeys[:, 0, :], src.rearrange("(p n) -> p n", p=EROWS)).then_inc(e_in, 16)
                    sp.dma_start(ekeys[:, 1, :], dst.rearrange("(p n) -> p n", p=EROWS)).then_inc(e_in, 16)

            def load_w(wc):
                w = w_parts[wc // 3][0]
                k = 2 * (wc % 3)
                if wc >= 2:
                    sp.wait_ge(w_lo, wc - 1)
                sp.dma_start(wst[:, wc % 2, :, :],
                             w[k * P:(k + 2) * P, :].rearrange("(k p) n -> p k n", p=P)).then_inc(w_in[wc % 2], 16)

            load_w(0)
            load_w(1)
            sp.dma_start(brow[:], b_qkv.rearrange("(c p) -> c p", p=P)).then_inc(b_in, 16)
            sp.wait_ge(keys, 1)
            sp.dma_start(keyd, key_t[:]).then_inc(key_out, 16)
            load_w(2)
            for s_ in (1, 0):
                sp.dma_start(ws[:, s_], w_qkv[:, s_ * D:s_ * D + P].rearrange("(k p) n -> p k n", p=P)
                             ).then_inc(wqk_in[s_], 16)
            sp.wait_ge(key_out, 16)

            def load_keys(u):
                if u >= 2:
                    sp.wait_ge(eq_done, u - 1)
                half, r0 = u // 5, (u % 5) * EC
                rows_of = keyd[r0:r0 + EC, half * T:(half + 1) * T]
                sp.dma_start(kb[:, u % 2, :, :], rows_of.unsqueeze(0).broadcast_to([T, EC, T])
                             ).then_inc(kb_in[u % 2], 16)

            load_keys(0)
            load_keys(1)
            for i in range(NT):
                sp.wait_ge(v_lo, 2 * i + 2)
                sp.dma_start(vdram[:, i, :].rearrange("(j p) f -> p j f", p=T),
                             VS[:, i % 2].bitcast(F32).rearrange("p (j a) l f -> p j (a l f)", a=2)
                             ).then_inc(v_store[i % 2], 16)
                if i + 2 < EU:
                    load_keys(i + 2)

        @block.gpsimd
        def _(pool):
            order = Chain(pool, pool_order)
            order(pool.memset(zeros[:], 0.0))
            order(pool.memset(ident[:], 0.0))
            order(pool.affine_select(out=ident[:], in_=ident[:], compare_op=ALU.not_equal, fill=1.0, base=0,
                                     pattern=[[-1, P]], channel_multiplier=1))
            order(pool.memset(triw[:], 1.0))
            order(pool.affine_select(out=triw[:], in_=triw[:], compare_op=ALU.is_ge, fill=1.0 + AGAIN, base=0,
                                     pattern=[[1, T]], channel_multiplier=-1))
            order(pool.memset(later[:], 1.0))
            order(pool.affine_select(out=later[:], in_=later[:], compare_op=ALU.is_gt, fill=0.0, base=0,
                                     pattern=[[1, T]], channel_multiplier=-1))
            order(pool.memset(blocks[:], 0.0))
            order(pool.memset(blocks[0:HD, 0:HD], 1.0))
            order(pool.memset(blocks[HD:P, HD:P], 1.0))
            order(pool.memset(ones2[:], 1.0))
            order(pool.iota(iota_i[:, 0:16], pattern=[[T, 16]], base=0, channel_multiplier=1))
            order(pool.iota(iota_i[:, 10:11], pattern=[[0, 1]], base=N * N, channel_multiplier=1))
            order(pool.iota(iota_i[:, 16:32], pattern=[[1, 16]], base=0, channel_multiplier=0))
            pool.tensor_copy(iota_f[:], iota_i[:]).then_inc(consts, 1)
            for i in range(NT):
                pool.wait_ge(x_in[i], 16)
            pool.wait_ge(w_in[1], 16)
            pool.dma_start(counts[0:N * N, :].rearrange("(s p d) o -> p s (d o)", p=T, d=N),
                           zeros[:].unsqueeze(1).broadcast_to([T, NT, N])).then_inc(scattered, 16)
            pool.dma_start(counts[N * N:N * N + T, :].rearrange("(a d) o -> a (d o)", a=1),
                           zeros[0:1, 0:T]).then_inc(scattered, 16)
            pool.wait_ge(key_out, 16)
            pool.wait_ge(w_in[0], 32)
            pool.dma_start(rows[0:SLOTS, :].rearrange("(p s) d -> p s d", p=120),
                           zeros[0:120, 0:D].unsqueeze(1).broadcast_to([120, 13, D])).then_inc(r_zero, 16)
            pool.dma_start(rows[SLOTS:, :].rearrange("(p s) d -> p s d", p=T),
                           zeros[:, 0:D].unsqueeze(1).broadcast_to([T, NT, D])).then_inc(r_zero, 16)
            pool.wait_ge(consts, 1)
            base = order.n
            with pool.Fori(0, EU) as u:
                pool.wait_ge(idx_ready, u + 1)
                for s in range(EC):
                    done = u * (2 * EC) + (base + 2 * s)
                    pool.tensor_copy(icur[:, s % 2:s % 2 + 1], idxf[:, at(u * EC + s, 1)]).then_inc(pool_order, 1)
                    pool.tensor_copy(vcur[:, s % 2:s % 2 + 1], countc[:, at(u * EC + s, 1)]).then_inc(pool_order, 1)
                    pool.wait_ge(pool_order, done + 2)
                    pool.wait_ge(scattered, u * (16 * EC) + (CLEARED + 16 * s))
                    pool.sem_inc(carrier, 1)
                    pool.indirect_dma_start(
                        out=counts, out_offset=bass.IndirectOffsetOnAxis(ap=icur[:, s % 2:s % 2 + 1], axis=0),
                        in_=vcur[:, s % 2:s % 2 + 1], in_offset=None, compute_op=ALU.add).then_inc(scattered, 16)
            pool.wait_ge(scattered, CLEARED + 16 * ET)

        @block.scalar
        def _(act):
            act.wait_ge(var_ready, 1)
            act.activation(rs[:, 1, :], rs[:, 0, :], ACT.Sqrt).then_inc(sd_ready, 1)

            def split_w(wc):
                act.wait_ge(w_in[wc % 2], 16 * (wc // 2 + 1))
                act.activation(wH[:, 2 * (wc % 3):2 * (wc % 3) + 2, :], wst[:, wc % 2, :, :], ACT.Copy).then_inc(w_hi, 1)

            for wc in range(3):
                split_w(wc)
            g = 0
            for t0, nt in GROUPS:
                for k in range(KT):
                    act.wait_ge(tr_done, g + 1)
                    act.activation(XH[:, k, t0 * T:(t0 + nt) * T], ps[:, g % 4, 0:nt * T], ACT.Copy).then_inc(xt_hi, 1)
                    g += 1
            for vg in range(2 * NT):
                i, c = vg // 2, vg % 2
                act.wait_ge(v_mm, vg + 1)
                if i >= 2:
                    act.wait_ge(v_store[i % 2], 16 * (i // 2))
                act.activation(VS[:, i % 2, 6 * c:6 * c + 6, 0, :],
                               ps[0:T, 4 + vg % 4, 0:HALF].rearrange("p (h f) -> p h f", h=6), ACT.Copy).then_inc(v_hi, 1)

        @block.vector
        def _(dve):
            order = Chain(dve, dve_order)
            dve.wait_ge(e_in, 32)
            dve.scalar_tensor_tensor(out=key_t[:], in0=ekeys[:, 0, :], scalar=float(N), in1=ekeys[:, 1, :],
                                     op0=ALU.mult, op1=ALU.add).then_inc(keys, 1)
            for i in range(NT):
                dve.wait_ge(x_in[i], 16)
                for c in range(2):
                    dve.bn_stats(stats[:, i, c, :], xn[:, i, c * HALF:(c + 1) * HALF]).then_inc(st_done, 1)
                if i >= 1:
                    dve.wait_ge(st_done, 2 * i)
                    dve.bn_aggr(mv[:, i - 1, :], stats[:, i - 1])
            dve.wait_ge(st_done, 2 * NT)
            order(dve.bn_aggr(mv[:, NT - 1, :], stats[:, NT - 1]))
            dve.tensor_scalar(rs[:, 0, :], mv[:, :, 1], EPS, None, ALU.add).then_inc(var_ready, 1)
            dve.wait_ge(var_ready, 1)
            dve.wait_ge(sd_ready, 1)
            order(dve.reciprocal(rs[:, 2, :], rs[:, 1, :]))
            order(dve.tensor_tensor(rs[:, 3, :], rs[:, 2, :], rs[:, 2, :], ALU.mult))
            order(dve.tensor_tensor(rs[:, 3, :], rs[:, 3, :], rs[:, 0, :], ALU.mult))
            order(dve.tensor_scalar(rs[:, 3, :], rs[:, 3, :], -0.5, 1.5, ALU.mult, ALU.add))
            order(dve.tensor_tensor(rs[:, 3, :], rs[:, 3, :], rs[:, 2, :], ALU.mult))
            for i in range(NT):
                dve.tensor_scalar(xn[:, i, :], xn[:, i, :], mv[:, i, 0:1], rs[:, 3, i:i + 1],
                                  ALU.subtract, ALU.mult).then_inc(xn_done, 1)

            def split_w(wc):
                dve.wait_ge(w_hi, wc + 1)
                k = 2 * (wc % 3)
                dve.tensor_tensor(wL[:, k:k + 2, :], wst[:, wc % 2, :, :], wH[:, k:k + 2, :].bitcast(F32),
                                  ALU.subtract).then_inc(w_lo, 1)

            def edge_chunk(u):
                dve.wait_ge(kb_in[u % 2], 16 * (u // 2 + 1))
                for s in range(EC):
                    c = u * EC + s
                    ins = dve.scalar_tensor_tensor(out=kb[:, u % 2, s, :], in0=kb[:, u % 2, s, :],
                                                   scalar=keyc[:, c:c + 1], in1=triw[:], op0=ALU.is_equal,
                                                   op1=ALU.mult, accum_out=countc[:, c:c + 1])
                order(ins)
                cs = slice(u * EC, (u + 1) * EC)
                order(dve.tensor_scalar(etmp[:, 0, :], countc[:, cs], AGAIN, None, ALU.is_ge))
                order(dve.tensor_scalar(etmp[:, 1, :], keyc[:, cs], -1.0, iota_f[:, 10:11], ALU.mult, ALU.add))
                order(dve.tensor_tensor(etmp[:, 2, :], etmp[:, 0, :], etmp[:, 1, :], ALU.mult))
                ins = dve.tensor_tensor(idxf[:, cs], etmp[:, 2, :], keyc[:, cs], ALU.add)
                ins.then_inc(idx_ready, 1)
                dve.wait_ge(idx_ready, u + 1)
                dve.sem_inc(eq_done, 1)

            for wc in range(2):
                split_w(wc)
            g = 0
            for t0, nt in GROUPS:
                for k in range(KT):
                    dve.wait_ge(xt_hi, g + 1)
                    dve.tensor_tensor(XL[:, k, t0 * T:(t0 + nt) * T], ps[:, g % 4, 0:nt * T],
                                      XH[:, k, t0 * T:(t0 + nt) * T].bitcast(F32), ALU.subtract).then_inc(xt_lo, 1)
                    g += 1
                if t0 == 0:
                    dve.wait_ge(key_tr, 1)
                    order(dve.memset(bcols[:, :, PAIRS:], 0.0))
                    bias = ps[:, 7, ET:ET + 3 * PAIRS].rearrange("p (s j) -> p s j", s=3)
                    dve.tensor_copy(bcols[:, 1:3, 0:PAIRS], bias[:, 1:3, :]).then_inc(keyc_done, 1)
                    dve.tensor_scalar(bcols[:, 0, 0:PAIRS], bias[:, 0, :], SCALE, None, ALU.mult).then_inc(keyc_done, 1)
                    dve.tensor_copy(keyc[:], ps[0:T, 7, 0:ET]).then_inc(keyc_done, 1)
                    dve.wait_ge(keyc_done, 3)
                    dve.wait_ge(consts, 1)
                    split_w(2)
                    edge_chunk(0)
            for vg in range(2 * NT):
                i, c = vg // 2, vg % 2
                dve.wait_ge(v_hi, vg + 1)
                dve.tensor_tensor(VS[:, i % 2, 6 * c:6 * c + 6, 1, :],
                                  ps[0:T, 4 + vg % 4, 0:HALF].rearrange("p (h f) -> p h f", h=6),
                                  VS[:, i % 2, 6 * c:6 * c + 6, 0, :].bitcast(F32), ALU.subtract).then_inc(v_lo, 1)
                if vg % 2 == 1 and vg // 2 < EU - 1:
                    edge_chunk(1 + vg // 2)

        @block.tensor
        def _(pe):
            pe.wait_ge(consts, 1)
            g = 0
            for t0, nt in GROUPS:
                pe.wait_ge(xn_done, t0 + nt)
                for k in range(KT):
                    if g >= 4:
                        pe.wait_ge(xt_lo, g - 3)
                    for t in range(nt):
                        ins = pe.transpose(ps[:, g % 4, t * T:(t + 1) * T], xn[:, t0 + t, k * P:(k + 1) * P],
                                           ident[0:T, 0:T])
                    ins.then_inc(tr_done, 1)
                    g += 1
                if t0 == 0:
                    pe.wait_ge(keys, 1)
                    for half in range(2):
                        ins = pe.transpose(ps[0:T, 7, half * EROWS:(half + 1) * EROWS],
                                           key_t[:, half * T:(half + 1) * T], ident[0:EROWS, 0:EROWS])
                    pe.wait_ge(b_in, 16)
                    ins = pe.transpose(ps[:, 7, 2 * EROWS:2 * EROWS + 3 * PAIRS], brow[:], ident[0:3 * PAIRS, 0:3 * PAIRS])
                    ins.then_inc(key_tr, 1)
            pe.wait_ge(keyc_done, 3)
            for vg in range(2 * NT):
                i, c = vg // 2, vg % 2
                if vg == 0:
                    pe.wait_ge(w_lo, 3)
                    pe.wait_ge(xt_lo, 3 * KT)
                if vg >= 4:
                    pe.wait_ge(v_lo, vg - 3)
                ins = product(pe, ps[0:T, 4 + vg % 4, 0:HALF],
                              lambda k: (XH[:, k, i * T:(i + 1) * T], XL[:, k, i * T:(i + 1) * T]),
                              lambda k: (wH[:, k, c * HALF:(c + 1) * HALF], wL[:, k, c * HALF:(c + 1) * HALF]), KT)
                ins.then_inc(v_mm, 1)

        HI_ON_ACT = [i % 5 in (1, 3) or i in (0, 27, 29) for i in range(STEPS)]
        NA = sum(HI_ON_ACT)
        ND = STEPS - NA
        FREE = 1
        END = STEPS + LAG + 3
        QUAD_AT, TOTAL_AT, SPREAD_AT = (3, 5, 8), (11, 12, 13), (17, 18, 19)
        PROJ_AT, TURN_AT, GRAM_AT = (7, 13, 20, 24, 29), (24, 27, 30), 32
        SLICES = 3
        READ_AT = (11, 16, 23, 27, 32)
        OWN_READ_AT = 3
        SECOND_AT = (1, 3, 6, 9, 13, 18)
        FIRST_AT = (24, 25, 26, 28)
        LATE_AT = (2, 5)
        WSPLIT_AT = (11, 25)
        FINISH_AT = (30, 32, END - 1)

        def step(i):
            a, c, kp = i // 15, (i // 5) % 3, i % 5
            return a, c, kp, CHUNKS[c][0], CHUNKS[c][1]

        NEXT_AT = (18, 21, 24)

        def load_w3(sp, wc):
            w, k = w_parts[wc // 3][0], 2 * (wc % 3)
            if wc >= 5:
                sp.wait_ge(w_lo, wc - 1)
            sp.dma_start(wst3[:, wc % 2, :, :],
                         w[k * P:(k + 2) * P, :].rearrange("(k p) n -> p k n", p=P)).then_inc(w_in[wc % 2], 16)

        def hi_w3(act, wc):
            act.wait_ge(w_in[wc % 2], 16 * (wc // 2 + 1))
            to = wH3 if wc < 6 else wpH
            act.activation(to[:, 2 * (wc % 3):2 * (wc % 3) + 2, :], wst3[:, wc % 2, :, :], ACT.Copy).then_inc(w_hi, 1)

        def lo_w3(dve, wc):
            dve.wait_ge(w_hi, wc + 1)
            k = 2 * (wc % 3)
            hi = wH3 if wc < 6 else wpH
            dve.tensor_tensor(wL3[:, k:k + 2, :], wst3[:, wc % 2, :, :], hi[:, k:k + 2, :].bitcast(F32),
                              ALU.subtract).then_inc(w_lo, 1)

        def values_over(eng):
            eng.wait_ge(v_store[0], 80)
            eng.wait_ge(v_store[1], 80)
            eng.wait_ge(v_mm, 2 * NT)
            eng.wait_ge(idx_ready, EU)
            eng.wait_ge(scattered, CLEARED)
            eng.wait_ge(r_zero, 32)

        @block.sync
        def _(sp):
            def load_w(j, s_):
                sp.dma_start(ws[:, s_], w_qkv[:, at(j * P + s_ * D, P)].rearrange("(k p) n -> p k n", p=P)
                             ).then_inc(wqk_in[s_], 16)

            def load_v(j, a):
                sp.dma_start(vsb[:, :, a, :].bitcast(F32), vdram[at(j * T, T), :, a * P:(a + 1) * P]).then_inc(v_in[a], 16)

            def second_half(a, n):
                own, other = slice(a * HD, (a + 1) * HD), slice((1 - a) * HD, (2 - a) * HD)
                for done, part in ((k_hi[a], KH[a]), (k_lo[a], KL[a])):
                    sp.wait_ge(done, n)
                    sp.dma_start(part[other, :].bitcast(F32), part[own, :].bitcast(F32)).then_inc(k_twice, 16)

            sp.sem_inc(ohl_free, FREE)
            sp.wait_ge(wqk_lo, 1)
            load_w(1, 1)
            sp.wait_ge(wqk_lo, 2)
            load_w(1, 0)
            values_over(sp)
            load_v(0, 0)
            second_half(0, 3)

            def turn(j, last):
                sp.wait_ge(oacc_done, 6 * j + FREE)
                load_v(j, 1)
                if not last:
                    sp.wait_ge(wqk_lo, 2 * j + 3)
                    load_w(j + 2, 1)
                second_half(1, 3 * j + 3)
                if not last:
                    sp.wait_ge(wqk_lo, 2 * j + 4)
                    sp.sem_inc(carrier, 1)
                    load_w(j + 2, 0)
                    sp.wait_ge(pv_done, j * STEPS + STEPS // 2)
                    load_v(j + 1, 0)
                    second_half(0, 3 * j + 6)
                else:
                    sp.wait_ge(g_mm, PAIRS)
                    for wc in (3, 4, 5):
                        load_w3(sp, wc)
                sp.wait_ge(o_fin, 3 * j + 3)
                for l in range(2):
                    sp.dma_start(odram[at(j * P, P), :, l, :],
                                 OHL[:, l, :].bitcast(F32).rearrange("p (i t) -> p i t", t=T)).then_inc(o_store, 16)
                if not last:
                    sp.wait_ge(o_store, 32 * j + 32)
                    sp.sem_inc(ohl_free, 1)

            with sp.Fori(0, PAIRS - 1) as j:
                turn(j, False)
            turn(PAIRS - 1, True)

        @block.scalar
        def _(act):
            def split_w(jn, s_):
                act.wait_ge(wqk_in[s_], 16 * jn + 16)
                act.activation(wqkH[:, s_], ws[:, s_], ACT.Copy).then_inc(wqk_hi, 1)

            def read_kq(jn, g):
                c0, w = CHUNKS[g % 3]
                bank = ps[:, 7, 0:w]
                act.wait_ge(qk_mm, 6 * jn + (g + 1))
                if g < 3:
                    act.activation(K32[:, c0:c0 + w], bank, ACT.Identity, bias=pbias[:, 1:2],
                                   accum_out=k1[:, g:g + 1]).then_inc(kq_full, 1)
                else:
                    act.activation(Q32[:, c0:c0 + w], bank, ACT.Identity, bias=pbias[:, 0:1],
                                   scale=SCALE).then_inc(kq_full, 1)

            def hi_part(a, jn, g):
                c0, w = CHUNKS[g % 3]
                h = slice(a * HD, (a + 1) * HD)
                act.wait_ge(kq_full, 6 * jn + (g + 1))
                if g < 3:
                    act.activation(KH[a][h, c0:c0 + w], K32[h, c0:c0 + w], ACT.Copy).then_inc(k_hi[a], 1)
                else:
                    act.activation(MQ[a][h, c0:c0 + w], Q32[h, c0:c0 + w], ACT.Copy).then_inc(q_hi[a], 1)

            def turn_k(jn, n):
                t0, nt = GROUPS[n]
                act.wait_ge(kt_mm, 3 * jn + (n + 1))
                act.activation(kt2[:, t0:t0 + nt, 0, :],
                               ps[0:T, 6, 0:nt * P].rearrange("p (t f) -> p t f", f=P),
                               ACT.Copy).then_inc(kt_hi, 1)

            split_w(0, 1)
            split_w(0, 0)
            values_over(act)
            act.wait_ge(bias_ready, 1)
            for g in range(3):
                read_kq(0, g)
            split_w(1, 1)
            for n in range(3):
                turn_k(0, n)
            for g in range(3):
                hi_part(0, 0, g)
            for g in (3, 4):
                read_kq(0, g)
            hi_part(0, 0, 3)

            def turn(j, last):
                def round_weights(i):
                    w = step(i)[4]
                    act.wait_ge(sq_done, j * STEPS + (i + 1))
                    if i >= RING:
                        act.wait_ge(pv_done, j * STEPS + (i - RING + 1))
                    act.activation(Ph[:, i % RING, :, 0:w], Pf[:, i % RING, :, 0:w], ACT.Identity,
                                   bias=1.0).then_inc(p_hiA, 1)

                def fold_out(s):
                    w = CHUNKS[s % 3][1]
                    act.wait_ge(pv_done, j * STEPS + (5 * s + 5))
                    if s >= 2:
                        act.wait_ge(oacc_done, 6 * j + (s - 1 + FREE))
                    act.activation(tmpo[:, s % 2, 0:w], ps[HD:P, 4 + s % 2, 0:w], ACT.Copy).then_inc(tmp_done, 1)

                def widen_inverse():
                    act.wait_ge(inv_done, j + 1)
                    act.activation(R32[0:T, :].rearrange("p (i a f) -> p i a f", a=2, f=HD),
                                   inv[:].unsqueeze(3).broadcast_to([T, NT, 2, HD]), ACT.Copy).then_inc(inv_wide, 1)

                def keep_inverse(c):
                    c0, w = CHUNKS[c]
                    act.wait_ge(inv_mm, 3 * j + (c + 1))
                    act.activation(rden[:, c0:c0 + w], ps[:, 6 + c % 2, 0:w], ACT.Copy).then_inc(rden_done, 1)

                for i in range(END):
                    if i < STEPS:
                        w = step(i)[4]
                        act.wait_ge(sc_done, j * STEPS + (i + 1))
                        if i >= RING:
                            act.wait_ge(p_lo, j * STEPS + (i - RING + 1))
                        act.activation(Pf[:, i % RING, :, 0:w], ps[0:T, 2 * (i % 2):2 * (i % 2) + 2, 0:w],
                                       ACT.Square, bias=1.0).then_inc(sq_done, 1)
                    if 1 <= i <= STEPS and HI_ON_ACT[i - 1]:
                        round_weights(i - 1)
                    if i == OWN_READ_AT:
                        read_kq(j, 5)
                    if i in SECOND_AT:
                        hi_part(1, j, SECOND_AT.index(i))
                    if i in LATE_AT:
                        hi_part(0, j, 4 + LATE_AT.index(i))
                    if i % 5 == 3 and i >= 8:
                        fold_out(i // 5 - 1)
                    if i == TOTAL_AT[2] + 2:
                        widen_inverse()
                    if i - 1 in SPREAD_AT:
                        keep_inverse(SPREAD_AT.index(i - 1))
                    if last and i in NEXT_AT:
                        if i == NEXT_AT[0]:
                            act.wait_ge(wqk_lo, 2 * PAIRS + 1)
                            act.wait_ge(wqk_in[0], 16 * (PAIRS + 1))
                        hi_w3(act, 3 + NEXT_AT.index(i))
                    if not last:
                        if i in WSPLIT_AT:
                            s_ = WSPLIT_AT.index(i)
                            split_w(j + (s_ + 1), s_)
                        if i in READ_AT:
                            g = READ_AT.index(i)
                            if g == 0:
                                act.wait_ge(k_lo[1], 3 * j + 3)
                                act.wait_ge(bias_ready, j + 2)
                            if g == 3:
                                act.wait_ge(r_done, 3 * j + 3)
                                act.wait_ge(q_lo[1], 3 * j + 3)
                            read_kq(j + 1, g)
                        if i - 1 in TURN_AT:
                            turn_k(j + 1, TURN_AT.index(i - 1))
                        if i in FIRST_AT:
                            hi_part(0, j + 1, FIRST_AT.index(i))

            with act.Fori(0, PAIRS - 1) as j:
                turn(j, False)
            turn(PAIRS - 1, True)

        @block.vector
        def _(dve):
            def split_w(jn, s_):
                dve.wait_ge(wqk_hi, 2 * jn + (2 - s_))
                dve.tensor_tensor(wqkL[:, s_], ws[:, s_], wqkH[:, s_].bitcast(F32), ALU.subtract).then_inc(wqk_lo, 1)

            def pair_bias(jn):
                dve.tensor_scalar(pbias[:], bcols[:, 0:2, at(jn, 1)].rearrange("p s o -> p (s o)"), 1.0, None,
                                  ALU.mult).then_inc(bias_ready, 1)

            def lo_part(a, jn, g):
                own, other = slice(a * HD, (a + 1) * HD), slice((1 - a) * HD, (2 - a) * HD)
                c0, w = CHUNKS[g % 3]
                cs, n = slice(c0, c0 + w), 3 * jn + (g % 3 + 1)
                if g < 3:
                    dve.wait_ge(k_hi[a], n)
                    dve.tensor_tensor(KL[a][own, cs], K32[own, cs], KH[a][own, cs].bitcast(F32),
                                      ALU.subtract).then_inc(k_lo[a], 1)
                else:
                    dve.wait_ge(q_hi[a], n)
                    dve.tensor_tensor(MQ[a][other, cs], Q32[own, cs], MQ[a][own, cs].bitcast(F32),
                                      ALU.subtract).then_inc(q_lo[a], 1)

            def sum_k(order):
                order(dve.tensor_reduce(k1[:, 3:4], k1[:, 0:3], AX.X, ALU.add))
                order(dve.tensor_scalar(k1[:, 3:4], k1[:, 3:4], 2.0, None, ALU.mult))

            def turn_k(jn, n):
                t0, nt = GROUPS[n]
                dve.wait_ge(kt_hi, 3 * jn + (n + 1))
                dve.tensor_tensor(kt2[:, t0:t0 + nt, 1, :],
                                  ps[0:T, 6, 0:nt * P].rearrange("p (t f) -> p t f", f=P),
                                  kt2[:, t0:t0 + nt, 0, :].bitcast(F32), ALU.subtract).then_inc(kt_lo, 1)

            def gram(order, jn):
                dve.wait_ge(g_mm, jn + 1)
                order(dve.tensor_scalar(gs[:, 0, :], ps[:, 6, P:2 * P], 2.0, None, ALU.mult))
                order(dve.tensor_tensor(gs[:, 1, :], ps[:, 6, 0:P], gs[:, 0, :], ALU.add))
                dve.tensor_tensor(gs[:, 2, :], gs[:, 1, :], blocks[:], ALU.mult).then_inc(gfin_done, 1)

            split_w(0, 1)
            split_w(0, 0)
            pair_bias(0)
            dve.sem_inc(oacc_done, FREE)
            values_over(dve)
            before = Chain(dve, pair_order)
            split_w(1, 1)
            for n in range(3):
                turn_k(0, n)
            for g in range(3):
                lo_part(0, 0, g)
            sum_k(before)
            gram(before, 0)
            lo_part(0, 0, 3)
            BEFORE, PER_PAIR = before.n, 1 + 6 + 2 + 2

            def turn(j, last):
                order = Chain(dve, pair_order, j * PER_PAIR + BEFORE)

                def quadratic(c):
                    c0, w = CHUNKS[c]
                    dve.wait_ge(gq_mm, 3 * j + (c + 1))
                    dve.scalar_tensor_tensor(out=R32[:, c0:c0 + w], in0=ps[:, 6 + c % 2, 0:w], scalar=k1[:, 3:4],
                                             in1=Q32[:, c0:c0 + w], op0=ALU.add, op1=ALU.mult).then_inc(r_done, 1)

                def inverse():
                    dve.wait_ge(den_mm, j + 1)
                    order(dve.tensor_scalar(inv[:].rearrange("p i a -> p (i a)"), ps[0:T, 6, 0:2 * NT], 2.0 * N, None,
                                            ALU.add))
                    dve.reciprocal(inv[:], inv[:]).then_inc(inv_done, 1)

                def fold_out(s):
                    a, (c0, w) = s // 3, CHUNKS[s % 3]
                    dve.wait_ge(tmp_done, 6 * j + (s + 1))
                    dve.tensor_tensor(OUN[a * HD:(a + 1) * HD, c0:c0 + w], ps[0:HD, 4 + s % 2, 0:w],
                                      tmpo[:, s % 2, 0:w], ALU.add).then_inc(oacc_done, 1)

                def finish(c):
                    c0, w = CHUNKS[c]
                    cs = slice(c0, c0 + w)
                    bv = bcols[:, 2, at(j, 1)]
                    dve.wait_ge(oacc_done, 6 * j + (4 + c + FREE))
                    dve.wait_ge(rden_done, 3 * j + (c + 1))
                    order(dve.tensor_tensor(R32[:, cs], OUN[:, cs], rden[:, cs], ALU.mult))
                    if c == 0:
                        dve.wait_ge(ohl_free, j + FREE)
                    order(dve.tensor_scalar(OHL[:, 0, cs], R32[:, cs], bv, None, ALU.add))
                    dve.scalar_tensor_tensor(out=OHL[:, 1, cs], in0=R32[:, cs], scalar=bv,
                                             in1=OHL[:, 0, cs].bitcast(F32), op0=ALU.add, op1=ALU.subtract
                                             ).then_inc(o_fin, 1)

                for i in range(END):
                    if i - 1 in QUAD_AT:
                        quadratic(QUAD_AT.index(i - 1))
                    if not last and i - 2 in TURN_AT:
                        turn_k(j + 1, TURN_AT.index(i - 2))
                    if i < STEPS:
                        w = step(i)[4]
                        p, f, h = Pl[:, i % RING, :, 0:w], Pf[:, i % RING, :, 0:w], Ph[:, i % RING, :, 0:w]
                        if i >= RING:
                            dve.wait_ge(pv_done, j * STEPS + (i - RING + 1))
                        if HI_ON_ACT[i]:
                            dve.wait_ge(p_hiA, j * NA + (sum(HI_ON_ACT[:i]) + 1))
                        else:
                            dve.wait_ge(sq_done, j * STEPS + (i + 1))
                            dve.tensor_scalar(h, f, 1.0, None, ALU.add).then_inc(p_hiD, 1)
                            dve.wait_ge(p_hiD, j * ND + (i - sum(HI_ON_ACT[:i]) + 1))
                        dve.scalar_tensor_tensor(out=p, in0=f, scalar=1.0, in1=h.bitcast(F32), op0=ALU.add,
                                                 op1=ALU.subtract).then_inc(p_lo, 1)
                    if i in SECOND_AT:
                        lo_part(1, j, SECOND_AT.index(i))
                    if i in LATE_AT:
                        lo_part(0, j, 4 + LATE_AT.index(i))
                    if i - 1 == TOTAL_AT[2]:
                        inverse()
                    if i % 5 == 4 and i >= 9:
                        fold_out(i // 5 - 1)
                    if last and i - 1 in NEXT_AT:
                        lo_w3(dve, 3 + NEXT_AT.index(i - 1))
                    if not last:
                        if i - 1 in WSPLIT_AT:
                            s_ = WSPLIT_AT.index(i - 1)
                            split_w(j + (s_ + 1), s_)
                        if i == PROJ_AT[0]:
                            dve.wait_ge(kq_full, 6 * j + 6)
                            pair_bias(j + 1)
                        if i - 1 in FIRST_AT:
                            g = FIRST_AT.index(i - 1)
                            lo_part(0, j + 1, g)
                            if g == 2:
                                sum_k(order)
                        if i - 1 == GRAM_AT:
                            gram(order, j + 1)
                    if i in FINISH_AT:
                        finish(FINISH_AT.index(i))
                dve.wait_ge(o_fin, 3 * j + 3)
                if not last:
                    assert order.n == PER_PAIR, order.n

            with dve.Fori(0, PAIRS - 1) as j:
                turn(j, False)
            turn(PAIRS - 1, True)

        @block.tensor
        def _(pe):
            def project(jn, g, k0=0, k1_=KT):
                s_, c = (1, g) if g < 3 else (0, g - 3)
                c0, w = CHUNKS[c]
                if k0 == 0:
                    project_waits(jn, g)
                ins = product(pe, ps[:, 7, 0:w], lambda k: (wqkH[:, s_, k, :], wqkL[:, s_, k, :]),
                              lambda k: (XH[:, k, c0:c0 + w], XL[:, k, c0:c0 + w]), KT, k0, k1_)
                if k1_ == KT:
                    ins.then_inc(qk_mm, 1)

            def project_waits(jn, g):
                if g == 0:
                    pe.wait_ge(wqk_lo, 2 * jn + 1)
                if g == 3:
                    pe.wait_ge(wqk_lo, 2 * jn + 2)
                if g > 0:
                    pe.wait_ge(kq_full, 6 * jn + g)

            def turn_k(jn, n):
                t0, nt = GROUPS[n]
                if n == 0:
                    pe.wait_ge(kq_full, 6 * jn + 3)
                else:
                    pe.wait_ge(kt_lo, 3 * jn + n)
                for t in range(nt):
                    ins = pe.transpose(ps[0:T, 6, t * P:(t + 1) * P],
                                       K32[:, (t0 + t) * T:(t0 + t + 1) * T], ident[:])
                ins.then_inc(kt_mm, 1)

            def gram(jn):
                pe.wait_ge(kt_lo, 3 * jn + 3)
                for t in range(NT):
                    ins = pe.matmul(ps[:, 6, 0:2 * P], kt2[:, t, 0, :], kt2[:, t].rearrange("p l f -> p (l f)"),
                                    start=(t == 0), stop=(t == NT - 1))
                ins.then_inc(g_mm, 1)

            pe.wait_ge(v_lo, 2 * NT)
            for g in range(3):
                project(0, g)
            for n in range(3):
                turn_k(0, n)
            project(0, 3)
            gram(0)
            project(0, 4)

            def turn(j, last):
                def quadratic(c):
                    c0, w = CHUNKS[c]
                    if c == 0:
                        pe.wait_ge(kq_full, 6 * j + 4)
                        pe.wait_ge(gfin_done, j + 1)
                    if c == 1:
                        pe.wait_ge(kq_full, 6 * j + 6)
                    if c == 2:
                        pe.wait_ge(r_done, 3 * j + 1)
                    pe.matmul(ps[:, 6 + c % 2, 0:w], gs[:, 2, :], Q32[:, c0:c0 + w], start=True,
                              stop=True).then_inc(gq_mm, 1)

                def total(n):
                    pe.wait_ge(r_done, 3 * j + 3)
                    t0, nt = GROUPS[n]
                    for t in range(t0, t0 + nt):
                        ins = pe.matmul(ps[0:T, 6, 2 * t:2 * t + 2], R32[:, t * T:(t + 1) * T], blocks[:, 0:P:HD],
                                        start=True, stop=True)
                    if n == 2:
                        ins.then_inc(den_mm, 1)

                def spread(c):
                    pe.wait_ge(inv_wide, j + 1)
                    if c == 1 and not last:
                        pe.wait_ge(kq_full, 6 * j + 8)
                    if c == 2:
                        pe.wait_ge(rden_done, 3 * j + 1)
                    c0, w = CHUNKS[c]
                    for t in range(NT):
                        s0, s1 = max(c0, t * T), min(c0 + w, (t + 1) * T)
                        if s0 < s1:
                            ins = pe.matmul(ps[:, 6 + c % 2, s0 - c0:s1 - c0],
                                            R32[0:T, t * P:(t + 1) * P],
                                            ident[0:T, s0 - t * T:s1 - t * T], start=True, stop=True)
                    ins.then_inc(inv_mm, 1)

                for i in range(STEPS + LAG + 1):
                    if i < STEPS:
                        a, c, kp, c0, w = step(i)
                        if i % 15 == 0:
                            pe.wait_ge(k_twice, 64 * j + 32 * (a + 1))
                        if i % 5 == 0:
                            pe.wait_ge(q_lo[a], 3 * j + (c + 1))
                        if i >= 2:
                            pe.wait_ge(sq_done, j * STEPS + (i - 1))
                        for t in range(2):
                            kt = 2 * kp + t
                            out_ = ps[0:T, 2 * (i % 2) + t, 0:w]
                            q = MQ[a][:, c0:c0 + w]
                            pe.matmul(out_, KH[a][:, kt * T:(kt + 1) * T], q, start=True, stop=False)
                            ins = pe.matmul(out_, KL[a][:, kt * T:(kt + 1) * T], q, start=False, stop=True)
                        ins.then_inc(sc_done, 1)
                    if LAG <= i < STEPS + LAG:
                        m = i - LAG
                        a, c, kp, c0, w = step(m)
                        s = m // 5
                        if m % 15 == 0:
                            pe.wait_ge(v_in[a], 16 * j + 16)
                        if m % 5 == 0 and s >= 2:
                            pe.wait_ge(oacc_done, 6 * j + (s - 1 + FREE))
                        elif m % 5 == 0:
                            pe.wait_ge(oacc_done, 6 * j + FREE)
                        pe.wait_ge(p_lo, j * STEPS + (m + 1))
                        for t in range(2):
                            for part in (Ph, Pl):
                                ins = pe.matmul(ps[:, 4 + s % 2, 0:w], vsb[:, 2 * kp + t, a, :],
                                                part[:, m % RING, t, 0:w], start=(kp == 0 and t == 0 and part is Ph),
                                                stop=(kp == 4 and t == 1 and part is Pl))
                        ins.then_inc(pv_done, 1)
                    if i in QUAD_AT:
                        quadratic(QUAD_AT.index(i))
                    if i in TOTAL_AT:
                        total(TOTAL_AT.index(i))
                    if i in SPREAD_AT:
                        spread(SPREAD_AT.index(i))
                    if i < SLICES:
                        project(j, 5, i * KT // SLICES, (i + 1) * KT // SLICES)
                    if not last and i >= PROJ_AT[0]:
                        g = max(g for g in range(5) if PROJ_AT[g] <= i)
                        part = i - PROJ_AT[g]
                        if i == PROJ_AT[0]:
                            pe.wait_ge(r_done, 3 * j + 2)
                        if i == PROJ_AT[2]:
                            pe.wait_ge(rden_done, 3 * j + 2)
                        if part < SLICES:
                            project(j + 1, g, part * KT // SLICES, (part + 1) * KT // SLICES)
                    if not last and i in TURN_AT:
                        if i == TURN_AT[0]:
                            pe.wait_ge(rden_done, 3 * j + 3)
                        turn_k(j + 1, TURN_AT.index(i))
                    if not last and i == GRAM_AT:
                        gram(j + 1)

            with pe.Fori(0, PAIRS - 1) as j:
                turn(j, False)
            turn(PAIRS - 1, True)

        steps_before = []

        def pairs_over(eng):
            eng.wait_ge(wqk_lo, 2 * PAIRS + 1)
            eng.wait_ge(wqk_in[0], 16 * (PAIRS + 1))
            eng.wait_ge(pv_done, PAIRS * STEPS)
            eng.wait_ge(tmp_done, 6 * PAIRS)
            eng.wait_ge(o_fin, 3 * PAIRS)

        @block.sync
        def _(sp):
            sp.dma_start(sbr[:], sb_.rearrange("(a d) -> a d", a=1).broadcast_to([T, E])).then_inc(bias_in, 16)
            sp.dma_start(swk[:], sw.rearrange("(k p) e -> p k e", p=P)).then_inc(bias_in, 16)
            pairs_over(sp)
            sp.dma_start(bgp[:], gnn_b.rearrange("(a d) -> a d", a=1).broadcast_to([T, D])).then_inc(bias_in, 16)

            def load_counts(q):
                if 2 <= q < NT + 2:
                    sp.wait_ge(csum_done, q - 1)
                if q >= NT + 2:
                    sp.wait_ge(csc_done, q - NT - 1)
                d = q % NT
                sp.dma_start(Cs[:, q % 2], counts[0:N * N].rearrange("(s p d) o -> p s (d o)", p=T, d=N)[
                    :, :, d * T:(d + 1) * T]).then_inc(cs_in[q % 2], 16)

            sp.wait_ge(scattered, CLEARED + 16 * ET)
            for q in range(NT):
                load_counts(q)
                if q in (2, 3):
                    load_w3(sp, 4 + q)
            sp.wait_ge(h_mm, 2 * NT)
            load_counts(NT)
            sp.wait_ge(o_store, 32 * PAIRS)
            for i in range(NT):
                if i + 1 < NT:
                    load_counts(NT + i + 1)
                sp.dma_start(xr[:, i % 2, :], x[i * T:(i + 1) * T, :]).then_inc(xr_in[i % 2], 16)
                if i == 0:
                    sp.dma_start(t0_[:, 1, :], b_proj.rearrange("(a d) -> a d", a=1).broadcast_to([T, D])
                                 ).then_inc(bias_in, 16)
                if i >= 1:
                    sp.wait_ge(pj_mm, i)
                sp.dma_start(oS[:].bitcast(F32).rearrange("p j l t -> p j (l t)"),
                             odram.rearrange("(j p) i l t -> p j i (l t)", p=P)[:, :, i, :]).then_inc(os_in, 16)
                if i == 0:
                    load_w3(sp, 8)
                if i >= 1:
                    sp.wait_ge(x1_done, i)
                    sp.dma_start(x1d[(i - 1) * T:i * T, :], t0_[:, (i - 1) % 2, :]).then_inc(x1_store[(i - 1) % 2], 16)
            sp.wait_ge(x1_done, NT)
            sp.dma_start(x1d[(NT - 1) * T:, :], t0_[:, (NT - 1) % 2, :]).then_inc(x1_store[(NT - 1) % 2], 16)

        @block.scalar
        def _(act):
            pairs_over(act)

            for g in range(2 * NT):
                i, c = g // 2, g % 2
                act.wait_ge(h_mm, g + 1)
                act.activation(HH[:, i, c * HALF:(c + 1) * HALF], ps[0:T, g % 4, 0:HALF], ACT.Copy).then_inc(h_hi, 1)
                if g == 11:
                    act.wait_ge(o_store, 32 * PAIRS)
                if g in (11, 13):
                    hi_w3(act, 6 + (g - 11) // 2)
            act.wait_ge(var_ready, 2)
            act.activation(dtmp[:, 1, :], dtmp[:, 0, :], ACT.Sqrt).then_inc(dinv_sd, 1)

            def evac_xf(i):
                act.wait_ge(xf_tr, i + 1)
                if i >= 1:
                    act.wait_ge(lg_mm, i)
                act.activation(xfT[:, 0:4, :], ps[:, 6, 0:4 * T].rearrange("p (k t) -> p k t", t=T), ACT.Copy
                               ).then_inc(xf_evac, 1)
                act.activation(xfT[:, 4:6, :], ps[:, 7, 0:2 * T].rearrange("p (k t) -> p k t", t=T), ACT.Copy
                               ).then_inc(xf_evac, 1)

            def round_counts(i):
                act.wait_ge(csc_done, i + 1)
                if i >= 2:
                    act.wait_ge(agg_mm, i - 1)
                act.activation(CH[:, i % 2], Csc[:], ACT.Copy).then_inc(ch_done, 1)

            round_counts(0)
            hi_w3(act, 8)
            for i in range(NT):
                if i + 1 < NT:
                    round_counts(i + 1)
                if i >= 1:
                    evac_xf(i - 1)
                act.wait_ge(var2, i + 1)
                act.activation(rs[:, 1, i:i + 1], rs[:, 0, i:i + 1], ACT.Sqrt).then_inc(sd2, 1)
            evac_xf(NT - 1)

        def newton(order, dve, r, sd, v, tmp):
            order(dve.reciprocal(r, sd))
            order(dve.tensor_tensor(tmp, r, r, ALU.mult))
            order(dve.tensor_tensor(tmp, tmp, v, ALU.mult))
            order(dve.tensor_scalar(tmp, tmp, -0.5, 1.5, ALU.mult, ALU.add))
            order(dve.tensor_tensor(r, r, tmp, ALU.mult))

        @block.vector
        def _(dve):
            pairs_over(dve)
            order = Chain(dve, route_order)

            for g in range(2 * NT):
                i, c = g // 2, g % 2
                cs = slice(c * HALF, (c + 1) * HALF)
                dve.wait_ge(h_hi, g + 1)
                dve.tensor_tensor(HL[:, i, cs], ps[0:T, g % 4, 0:HALF], HH[:, i, cs].bitcast(F32),
                                  ALU.subtract).then_inc(h_lo, 1)
                if c == 1:
                    dve.wait_ge(cs_in[i % 2], 16 * (i // 2 + 1))
                    if i >= 2:
                        dve.wait_ge(deg_mm, i - 1)
                    dve.tensor_reduce(csum[:, i % 2, :], Cs[:, i % 2].rearrange("p s d -> p d s"), AX.X,
                                      ALU.add).then_inc(csum_done, 1)
            dve.wait_ge(deg_mm, NT)
            dve.tensor_scalar(dtmp[:, 0, :], ps[0:T, 4, 0:2 * NT].rearrange("p (i a) -> p i a", a=2)[:, :, 0], 1.0, None,
                              ALU.add).then_inc(var_ready, 1)
            dve.wait_ge(dinv_sd, 1)
            newton(order, dve, dinv[:], dtmp[:, 1, :], dtmp[:, 0, :], dtmp[:, 2, :])

            def scale_counts(i):
                q = NT + i
                dve.wait_ge(cs_in[q % 2], 16 * (q // 2 + 1))
                order(dve.tensor_tensor(Cs[:, q % 2, i, :], Cs[:, q % 2, i, :], ident[0:T, 0:T], ALU.add))
                if i >= 1:
                    dve.wait_ge(cl_done, i)
                dve.tensor_tensor(Csc[:], Cs[:, q % 2], dinv[:].unsqueeze(2).broadcast_to([T, NT, T]),
                                  ALU.mult).then_inc(csc_done, 1)
                dve.wait_ge(ch_done, i + 1)
                if i >= 2:
                    dve.wait_ge(agg_mm, i - 1)
                dve.tensor_tensor(CL[:, i % 2], Csc[:], CH[:, i % 2].bitcast(F32), ALU.subtract).then_inc(cl_done, 1)

            def logits(i):
                dve.wait_ge(lg_mm, i + 1)
                dve.tensor_tensor(lg[:, 0, i, :], ps[0:T, 7, 384:384 + E], sbr[:], ALU.add).then_inc(lg_done, 1)

            scale_counts(0)
            for wc in (6, 7, 8):
                lo_w3(dve, wc)
            dve.wait_ge(bias_in, 64)
            order(dve.tensor_tensor(bgp[:], bgp[:], t0_[:, 1, :], ALU.add))
            for i in range(NT):
                t_ = t0_[:, i % 2, :]
                th = t_.rearrange("p (c n) -> p c n", c=2)
                if i >= 2:
                    dve.wait_ge(x1_store[i % 2], 16 * (i // 2))
                dve.wait_ge(xr_in[i % 2], 16 * (i // 2 + 1))
                order(dve.tensor_tensor(t_, xr[:, i % 2, :], bgp[:], ALU.add))
                dve.wait_ge(agg_mm, i + 1)
                b = 2 * (i % 2)
                dve.scalar_tensor_tensor(out=th, in0=ps[0:T, b:b + 2, 0:HALF], scalar=dinv[:, i:i + 1], in1=th,
                                         op0=ALU.mult, op1=ALU.add).then_inc(agg_read, 1)
                if i + 1 < NT:
                    scale_counts(i + 1)
                dve.wait_ge(agg_read, i + 1)
                dve.wait_ge(pj_mm, i + 1)
                dve.tensor_tensor(th, ps[0:T, 4:6, 0:HALF], th, ALU.add).then_inc(x1_done, 1)
                dve.wait_ge(x1_done, i + 1)
                for c in range(2):
                    dve.bn_stats(stats[:, i, c, :], t_[:, c * HALF:(c + 1) * HALF]).then_inc(st_done, 1)
                dve.wait_ge(st_done, 2 * NT + 2 * i + 2)
                order(dve.bn_aggr(mv[:, i, :], stats[:, i]))
                dve.tensor_scalar(rs[:, 0, i:i + 1], mv[:, i, 1:2], EPS, None, ALU.add).then_inc(var2, 1)
                if i >= 1:
                    logits(i - 1)
                dve.wait_ge(sd2, i + 1)
                newton(order, dve, rs[:, 2, i:i + 1], rs[:, 1, i:i + 1], rs[:, 0, i:i + 1], rs[:, 3, i:i + 1])
                dve.tensor_scalar(XF[:, i, :], t_, mv[:, i, 0:1], rs[:, 2, i:i + 1], ALU.subtract,
                                  ALU.mult).then_inc(xf_done, 1)
            logits(NT - 1)
            steps_before.append(order.n)

        @block.tensor
        def _(pe):
            pairs_over(pe)
            pe.wait_ge(oacc_done, 6 * PAIRS + FREE)
            pe.wait_ge(w_lo, 6)

            def degrees(i):
                pe.wait_ge(csum_done, i + 1)
                pe.matmul(ps[0:T, 4, 2 * i:2 * i + 2], csum[:, i % 2, :], ones2[:], start=True, stop=True
                          ).then_inc(deg_mm, 1)

            for g in range(2 * NT):
                i, c = g // 2, g % 2
                if g >= 4:
                    pe.wait_ge(h_lo, g - 3)
                product(pe, ps[0:T, g % 4, 0:HALF],
                        lambda k: (XH[:, k, i * T:(i + 1) * T], XL[:, k, i * T:(i + 1) * T]),
                        lambda k: (wH3[:, k, c * HALF:(c + 1) * HALF], wL3[:, k, c * HALF:(c + 1) * HALF]),
                        KT).then_inc(h_mm, 1)
                if c == 1 and i >= 1:
                    degrees(i - 1)
            degrees(NT - 1)

            def transposes(i):
                pe.wait_ge(xf_done, i + 1)
                if i >= 1:
                    pe.wait_ge(lg_done, i)
                for k in range(KT):
                    ins = pe.transpose(ps[:, 6 + k // 4, (k % 4) * T:(k % 4 + 1) * T], XF[:, i, k * P:(k + 1) * P],
                                       ident[0:T, 0:T])
                ins.then_inc(xf_tr, 1)

            def logits(i):
                pe.wait_ge(xf_evac, 2 * i + 2)
                for k in range(KT):
                    ins = pe.matmul(ps[0:T, 7, 384:384 + E], xfT[:, k, :], swk[:, k, :], start=(k == 0),
                                    stop=(k == KT - 1))
                ins.then_inc(lg_mm, 1)

            pe.wait_ge(dinv_sd, 1)
            pe.wait_ge(h_lo, 2 * NT)
            for i in range(NT):
                pe.wait_ge(cl_done, i + 1)
                if i >= 2:
                    pe.wait_ge(agg_read, i - 1)
                for c in range(2):
                    ins = product(pe, ps[0:T, 2 * (i % 2) + c, 0:HALF],
                                  lambda s: (CH[:, i % 2, s, :], CL[:, i % 2, s, :]),
                                  lambda s: (HH[:, s, c * HALF:(c + 1) * HALF], HL[:, s, c * HALF:(c + 1) * HALF]), NT)
                ins.then_inc(agg_mm, 1)
                if i >= 1:
                    transposes(i - 1)
                pe.wait_ge(os_in, 16 * i + 16)
                if i == 0:
                    pe.wait_ge(w_lo, 9)
                else:
                    pe.wait_ge(x1_done, i)
                for c in range(2):
                    ins = product(pe, ps[0:T, 4 + c, 0:HALF], lambda k: (oS[:, k, 0, :], oS[:, k, 1, :]),
                                  lambda k: (wpH[:, k, c * HALF:(c + 1) * HALF], wL3[:, k, c * HALF:(c + 1) * HALF]), KT)
                ins.then_inc(pj_mm, 1)
                if i >= 1:
                    logits(i - 1)
            transposes(NT - 1)
            logits(NT - 1)

        def nodes_over(eng):
            eng.wait_ge(agg_mm, NT)
            eng.wait_ge(pj_mm, NT)
            eng.wait_ge(lg_mm, NT)
            eng.wait_ge(cl_done, NT)
            eng.wait_ge(xf_done, NT)
            eng.wait_ge(lg_done, NT)
            eng.wait_ge(x1_store[0], 80)
            eng.wait_ge(x1_store[1], 80)

        LASTM = E // 2 - 1

        @block.sync
        def _(sp):
            def load_w1(e):
                sp.dma_start(w1s[:], w1.rearrange("e d f -> (e d) f")[at(e * D, D)].rearrange("(k p) f -> p k f", p=P)
                             ).then_inc(w_in[0], 16)

            def load_w2(e):
                sp.dma_start(w2s[:], w2.rearrange("e d f -> (e d) f")[at(e * F, F)].rearrange("(k p) f -> p k f", p=P)
                             ).then_inc(w_in[1], 16)

            def load_rows(e, b):
                for t, (r0, n) in enumerate(CTILES):
                    sp.dma_start(xe[0:n, b, t, :], rows[at(e * CAP + r0, n), :]).then_inc(xe_in[b], 16)

            def load_b2(e, b):
                sp.dma_start(b2r[:, b, :], b2[at(e, 1), :].broadcast_to([98, D])).then_inc(b2_in[b], 16)

            nodes_over(sp)
            sp.sem_inc(oe_store, FREE)
            sp.dma_start(b1row[:], b1.rearrange("e (m p) -> (e m) p", p=P)).then_inc(b1_in, 16)
            load_w1(0)
            load_w2(0)
            load_b2(0, 0)
            sp.wait_ge(we_lo, 1)
            load_w1(1)
            sp.wait_ge(we_lo, 2)
            load_w2(1)
            sp.wait_ge(sent, 16 * NT)
            load_rows(0, 0)
            load_rows(1, 1)

            def turn(m, last):
                for b in range(2):
                    e = 2 * m + b
                    if not last:
                        sp.wait_ge(xe_tr, 3 * e + 3)
                        load_rows(e + 2, b)
                    if not (last and b == 1):
                        load_b2(e + 1, 1 - b)
                    if not last:
                        sp.wait_ge(we_lo, 2 * e + 3)
                        sp.sem_inc(carrier, 1)
                        load_w1(e + 2)
                        sp.wait_ge(we_lo, 2 * e + 4)
                        sp.sem_inc(carrier, 1)
                        load_w2(e + 2)
                    for t, (r0, n) in enumerate(CTILES):
                        sp.wait_ge(oe_done, 2 * e + (t + 1 + FREE))
                        sp.dma_start(rows[at(e * CAP + r0, n), :], oE[0:n, t, :]).then_inc(oe_store, 16)

            with sp.Fori(0, LASTM) as m:
                turn(m, False)
            sp.dma_start(XF[:], x1d.rearrange("(i p) d -> p i d", p=T)).then_inc(x1_back, 16)
            turn(LASTM, True)

        @block.gpsimd
        def _(pool):
            pool.wait_ge(slot_done, 1)
            pool.wait_ge(xf_done, NT)
            pool.wait_ge(r_zero, 32)
            for i in range(NT):
                pool.indirect_dma_start(out=rows, out_offset=bass.IndirectOffsetOnAxis(ap=slots[:, i:i + 1], axis=0),
                                        in_=XF[:, i, :], in_offset=None).then_inc(sent, 16)

        @block.scalar
        def _(act):
            nodes_over(act)

            W1_BASE, W2_BASE = 80, 64

            def split_w1(e, b):
                act.wait_ge(w_in[0], W1_BASE + 16 + e * 16)
                act.activation(w1H[:, b], w1s[:], ACT.Copy).then_inc(we_hi, 1)

            def split_w2(e, b):
                act.wait_ge(w_in[1], W2_BASE + 16 + e * 16)
                act.activation(w2H[:, b], w2s[:], ACT.Copy).then_inc(we_hi, 1)

            act.wait_ge(dm_done, 1)
            act.activation(lg[:, 2], lg[:, 1], ACT.Exp).then_inc(ex_done, 1)
            for n, (t0, nt) in enumerate(GROUPS):
                act.wait_ge(pm_mm, n + 1)
                act.activation(PM[:, t0 * T:(t0 + nt) * T], ps[0:T, n, 0:nt * T], ACT.Copy).then_inc(pm_evac, 1)
            split_w1(0, 0)
            split_w2(0, 0)

            def cut_rows(e):
                for n in range(3):
                    act.wait_ge(xe_tr, 3 * e + (n + 1))
                    act.activation(xeH[:, 2 * n:2 * n + 2, 0:CAP],
                                   ps[:, n, 0:2 * CAPP].rearrange("p (k c) -> p k c", k=2)[:, :, 0:CAP],
                                   ACT.Copy).then_inc(xe_hi, 1)

            act.wait_ge(pads, 1)
            cut_rows(0)

            def turn(m, last):
                for b in range(2):
                    e = 2 * m + b
                    if not (last and b == 1):
                        split_w1(e + 1, 1 - b)
                    act.wait_ge(b1cur_done, e + 1)
                    for f in range(FT):
                        act.wait_ge(m1_mm, 3 * e + (f + 1))
                        act.activation(h32[:, f, :], ps[:, 3 + f, 0:CAPP], ACT.Gelu,
                                       bias=b1cur[:, b, f:f + 1]).then_inc(h_act, 1)
                        act.wait_ge(h_act, 3 * e + (f + 1))
                        act.activation(hH[:, f, :], h32[:, f, :], ACT.Copy).then_inc(hh_done, 1)
                    if not (last and b == 1):
                        cut_rows(e + 1)
                        split_w2(e + 1, 1 - b)

            with act.Fori(0, LASTM) as m:
                turn(m, False)
            turn(LASTM, True)

        @block.vector
        def _(dve):
            nodes_over(dve)
            order = Chain(dve, route_order, steps_before[0])

            def split_w1(e, b):
                dve.wait_ge(we_hi, 2 * e + 1)
                dve.tensor_tensor(w1L[:, b], w1s[:], w1H[:, b].bitcast(F32), ALU.subtract).then_inc(we_lo, 1)

            def split_w2(e, b):
                dve.wait_ge(we_hi, 2 * e + 2)
                dve.tensor_tensor(w2L[:, b], w2s[:], w2H[:, b].bitcast(F32), ALU.subtract).then_inc(we_lo, 1)

            def wide(a):
                return a.unsqueeze(2).broadcast_to([T, NT, E])

            top, pm, route, rank, kept, slot, slotf, tok, sm = (rt[:, n, :] for n in range(9))
            eid = iota_f[:, 16:16 + E].unsqueeze(1).broadcast_to([T, NT, E])
            order(dve.tensor_reduce(top, lg[:, 0], AX.X, ALU.max))
            dve.tensor_tensor(lg[:, 1], lg[:, 0], wide(top), ALU.subtract).then_inc(dm_done, 1)
            dve.wait_ge(dm_done, 1)
            order(dve.tensor_scalar(lg[:, 3], lg[:, 1], 0.0, None, ALU.is_ge))
            order(dve.scalar_tensor_tensor(out=lg[:, 4], in0=lg[:, 3], scalar=-100.0, in1=eid, op0=ALU.mult, op1=ALU.add))
            order(dve.tensor_reduce(route, lg[:, 4], AX.X, ALU.min))
            order(dve.tensor_scalar(route, route, 100.0, None, ALU.add))
            order(dve.tensor_tensor(lg[:, 3], eid, wide(route), ALU.is_equal))
            order(dve.tensor_copy(ohb[:], lg[:, 3]))
            dve.wait_ge(ex_done, 1)
            order(dve.tensor_reduce(sm, lg[:, 2], AX.X, ALU.add))
            dve.reciprocal(pm, sm).then_inc(pm_done, 1)
            dve.memset(xeH[:, :, CAP:].bitcast(F32), 0.0)
            dve.memset(xeL[:, :, CAP:].bitcast(F32), 0.0).then_inc(pads, 1)
            dve.wait_ge(pm_evac, len(GROUPS))
            for jt in range(NT):
                mine = pm[:, jt:jt + 1]
                lo, hi = jt * T, (jt + 1) * T
                dve.scalar_tensor_tensor(out=same[:, jt % 2, :], in0=PM[:, lo:hi], scalar=mine, in1=later[:],
                                         op0=ALU.is_equal, op1=ALU.mult).then_inc(same_done, 1)
                if jt > 0:
                    dve.tensor_scalar(Bt[:, jt, 0:lo], PM[:, 0:lo], mine, None, ALU.is_lt).then_inc(b_done, 1)
                if jt < NT - 1:
                    dve.tensor_scalar(Bt[:, jt, hi:], PM[:, hi:], mine, None, ALU.is_le).then_inc(b_done, 1)
                dve.wait_ge(same_done, jt + 1)
                dve.scalar_tensor_tensor(out=Bt[:, jt, lo:hi], in0=PM[:, lo:hi], scalar=mine, in1=same[:, jt % 2, :],
                                         op0=ALU.is_lt, op1=ALU.add).then_inc(b_done, 1)
            dve.wait_ge(cnt_mm, 1)
            order(dve.tensor_tensor(lg[:, 4], ps[0:T, 3, 0:NT * E].rearrange("p (i e) -> p i e", e=E), lg[:, 3], ALU.mult))
            order(dve.tensor_reduce(rank, lg[:, 4], AX.X, ALU.add))
            order(dve.tensor_scalar(kept, rank, float(CAP), None, ALU.is_lt))
            order(dve.scalar_tensor_tensor(out=slot, in0=route, scalar=float(CAP), in1=rank, op0=ALU.mult, op1=ALU.add))
            order(dve.tensor_scalar(tok, iota_f[:, 0:NT], float(SLOTS), None, ALU.add))
            order(dve.tensor_tensor(slot, slot, tok, ALU.subtract))
            order(dve.tensor_tensor(slot, slot, kept, ALU.mult))
            order(dve.tensor_tensor(slotf, slot, tok, ALU.add))
            dve.tensor_copy(slots[:], slotf).then_inc(slot_done, 1)
            split_w1(0, 0)
            split_w2(0, 0)
            dve.wait_ge(b1_tr, 1)
            dve.tensor_copy(b1c[:].rearrange("p e m -> p (e m)"), ps[:, 3, 256:256 + E * FT]).then_inc(b1_done, 1)
            dve.wait_ge(b1_done, 1)

            def bias_of(e, b):
                dve.tensor_scalar(b1cur[:, b, :], b1c[:, at(e, 1), :].rearrange("p o m -> p (o m)"), 1.0, None,
                                  ALU.mult).then_inc(b1cur_done, 1)

            def cut_rows(e):
                for n in range(3):
                    dve.wait_ge(xe_hi, 3 * e + (n + 1))
                    dve.tensor_tensor(xeL[:, 2 * n:2 * n + 2, 0:CAP],
                                      ps[:, n, 0:2 * CAPP].rearrange("p (k c) -> p k c", k=2)[:, :, 0:CAP],
                                      xeH[:, 2 * n:2 * n + 2, 0:CAP].bitcast(F32), ALU.subtract).then_inc(xe_lo, 1)

            dve.sem_inc(oe_done, FREE)
            bias_of(0, 0)
            cut_rows(0)

            def turn(m, last):
                for b in range(2):
                    e = 2 * m + b
                    if not (last and b == 1):
                        split_w1(e + 1, 1 - b)
                    for f in range(FT):
                        dve.wait_ge(hh_done, 3 * e + (f + 1))
                        dve.tensor_tensor(hL[:, f, :], h32[:, f, :], hH[:, f, :].bitcast(F32),
                                          ALU.subtract).then_inc(hl_done, 1)
                    if not (last and b == 1):
                        bias_of(e + 1, 1 - b)
                        cut_rows(e + 1)
                        split_w2(e + 1, 1 - b)
                    dve.wait_ge(b2_in[b], m * 16 + 16)
                    for t, (r0, n) in enumerate(CTILES):
                        dve.wait_ge(m2_mm, 2 * e + (t + 1))
                        dve.wait_ge(oe_store, 32 * e + FREE)
                        dve.tensor_tensor(oE[0:n, t, :].rearrange("p (c d) -> p c d", c=2),
                                          ps[0:n, 6 - 2 * t:8 - 2 * t, 0:HALF],
                                          b2r[0:n, b, :].rearrange("p (c d) -> p c d", c=2), ALU.add).then_inc(oe_done, 1)

            with dve.Fori(0, LASTM) as m:
                turn(m, False)
            turn(LASTM, True)

        @block.tensor
        def _(pe):
            nodes_over(pe)
            pe.wait_ge(b1_in, 16)
            pe.transpose(ps[:, 3, 256:256 + E * FT], b1row[:], ident[0:E * FT, 0:E * FT]).then_inc(b1_tr, 1)
            pe.wait_ge(pm_done, 1)
            for n, (t0, nt) in enumerate(GROUPS):
                for t in range(nt):
                    i = t0 + t
                    ins = pe.matmul(ps[0:T, n, t * T:(t + 1) * T], rt[:, 1, i:i + 1].broadcast_to([T, T]),
                                    ident[0:T, 0:T], start=True, stop=True)
                ins.then_inc(pm_mm, 1)
            for jt in range(NT):
                pe.wait_ge(b_done, 3 * jt + (2 if jt < NT - 1 else 1))
                for i in range(NT):
                    ins = pe.matmul(ps[0:T, 3, i * E:(i + 1) * E], Bt[:, jt, i * T:(i + 1) * T], ohb[:, jt, :],
                                    start=(jt == 0 and i == 0), stop=(jt == NT - 1 and i == NT - 1))
            ins.then_inc(cnt_mm, 1)

            def turn_rows(e, b, n_in):
                pe.wait_ge(xe_in[b], n_in)
                for n in range(3):
                    for k in range(2):
                        for t, (r0, cnt) in enumerate(CTILES):
                            f = 2 * n + k
                            ins = pe.transpose(ps[:, n, k * CAPP + r0:k * CAPP + r0 + cnt],
                                               xe[0:cnt, b, t, f * P:(f + 1) * P], ident[0:cnt, 0:cnt])
                    ins.then_inc(xe_tr, 1)

            turn_rows(0, 0, 32)

            def turn(m, last):
                for b in range(2):
                    e = 2 * m + b
                    pe.wait_ge(xe_lo, 3 * e + 3)
                    pe.wait_ge(we_lo, 2 * e + 1)
                    for f in range(FT):
                        if f == 0:
                            pe.wait_ge(b1_done, 1)
                        elif f == 1:
                            pe.wait_ge(oe_done, 2 * e + FREE)
                        product(pe, ps[:, 3 + f, 0:CAPP],
                                lambda k: (w1H[:, b, k, f * P:(f + 1) * P], w1L[:, b, k, f * P:(f + 1) * P]),
                                lambda k: (xeH[:, k, :], xeL[:, k, :]), KT).then_inc(m1_mm, 1)
                    if not (last and b == 1):
                        turn_rows(e + 1, 1 - b, m * 32 + 32 * (b + 1))
                    pe.wait_ge(hl_done, 3 * e + 3)
                    pe.wait_ge(we_lo, 2 * e + 2)
                    for t, (r0, n) in enumerate(CTILES):
                        for c in range(2):
                            ins = product(pe, ps[0:n, 6 - 2 * t + c, 0:HALF],
                                          lambda f: (hH[:, f, r0:r0 + n], hL[:, f, r0:r0 + n]),
                                          lambda f: (w2H[:, b, f, c * HALF:(c + 1) * HALF],
                                                     w2L[:, b, f, c * HALF:(c + 1) * HALF]), FT)
                        ins.then_inc(m2_mm, 1)

            with pe.Fori(0, LASTM) as m:
                turn(m, False)
            turn(LASTM, True)

        @block.sync
        def _(sp):
            sp.wait_ge(sent, 16 * NT)
            for i in range(NT):
                sp.wait_ge(out_done, i + 1)
                sp.dma_start(out[i * T:(i + 1) * T, :], yg[:, i, :]).then_inc(stored, 16)
            sp.wait_ge(stored, 16 * NT)
            sp.wait_ge(oe_store, 32 * E + FREE)

        @block.gpsimd
        def _(pool):
            pool.wait_ge(oe_store, 32 * E + FREE)
            pool.wait_ge(we_lo, 2 * E)
            pool.wait_ge(m2_mm, 2 * E)
            for i in range(NT):
                pool.indirect_dma_start(out=yg[:, i, :], out_offset=None, in_=rows,
                                        in_offset=bass.IndirectOffsetOnAxis(ap=slots[:, i:i + 1], axis=0)
                                        ).then_inc(got[GOT[i]], 16)

        @block.vector
        def _(dve):
            dve.wait_ge(x1_back, 16)
            for i in range(NT):
                dve.wait_ge(got[GOT[i]], 16 * GOT.count(GOT[i]))
                dve.scalar_tensor_tensor(out=yg[:, i, :], in0=yg[:, i, :], scalar=rt[:, 1, i:i + 1], in1=XF[:, i, :],
                                         op0=ALU.mult, op1=ALU.add).then_inc(out_done, 1)


def product(pe, out, left, right, tiles, first=0, end=None):
    for k in range(first, tiles if end is None else end):
        lh, ll = left(k)
        rh, rl = right(k)
        pe.matmul(out, lh, rh, start=(k == 0), stop=False)
        pe.matmul(out, lh, rl, start=False, stop=False)
        ins = pe.matmul(out, ll, rh, start=False, stop=(k == tiles - 1))
    return ins


_INS = ["x", "src", "dst", "L0_gnn_W", "L0_gnn_b", "L0_mix_w_qkv", "L0_mix_b_qkv", "L0_mix_w_proj",
        "L0_mix_b_proj", "L0_ffn_switch_w", "L0_ffn_switch_b", "L0_ffn_w1", "L0_ffn_b1", "L0_ffn_w2",
        "L0_ffn_b2"]


def kernel(**inputs):
    import numpy as _np
    import concourse.bacc as _bacc
    from concourse.bass_utils import run_bass_kernel_spmd as _run

    nc = _bacc.Bacc("TRN2", target_bir_lowering=False, num_devices=1)
    arrays, args = {}, []
    for name in _INS:
        a = _np.ascontiguousarray(inputs[name])
        arrays[name] = a
        args.append(nc.dram_tensor(name, a.shape, mybir.dt.from_np(a.dtype), kind="ExternalInput").ap())
    result = nc.dram_tensor("out", (N, D), F32, kind="ExternalOutput").ap()
    counts = nc.dram_tensor("counts", (N * N + T, 1), F32, kind="Internal").ap()
    keyd = nc.dram_tensor("keyd", (EROWS, 250), F32, kind="Internal").ap()
    vdram = nc.dram_tensor("vdram", (PAIRS * T, NT, 4 * HD), F32, kind="Internal").ap()
    odram = nc.dram_tensor("odram", (PAIRS * P, NT, 2, T), F32, kind="Internal").ap()
    rows = nc.dram_tensor("rows", (SLOTS + N, D), F32, kind="Internal").ap()
    x1d = nc.dram_tensor("x1d", (N, D), F32, kind="Internal").ap()
    build(nc, *args, result, counts, keyd, vdram, odram, rows, x1d)
    return _run(nc, [arrays], core_ids=[0]).results[0]["out"]
```
